# Optimizing a Trainium2 kernel written in Bass

```python
import numpy as np
import jax
import jax.numpy as jnp

def _softmax(x, axis=-1):
    return jax.nn.softmax(x, axis=axis)

def _gelu(x):
    return jax.nn.gelu(x, approximate=True)

def _silu(x):
    return jax.nn.silu(x)

def _sigmoid(x):
    return jax.nn.sigmoid(x)

def _layernorm(x, axis=-1, eps=1e-05):
    m = jnp.mean(x, axis=axis, keepdims=True)
    v = jnp.var(x, axis=axis, keepdims=True)
    return (x - m) / jnp.sqrt(v + eps)

def _scatter_add(tgt, idx, src, axis=0):
    return tgt.at[idx].add(src)

def _segment_sum(src, seg, n):
    return jax.ops.segment_sum(src, seg, n)
kernel_name = 'mk_decoder_preln_d2_seqx_r8_d3967c'

def setup_inputs(seed: int=0):
    np.random.seed(seed)
    _w = jnp.asarray

    def _rec_inputs():
        import jax
        import jax.numpy as jnp
        _rk = jax.random.key(seed)
        x = -0.0002928 + 1 * jax.random.normal(jax.random.fold_in(_rk, 1), (8, 128, 256), jnp.float32)
        _lenS = 128 - jax.random.randint(jax.random.fold_in(_rk, 7), (8,), 0, max(1, 128 // 4) + 1, jnp.int32)
        _lenS2 = 128 - jax.random.randint(jax.random.fold_in(_rk, 8), (8,), 0, max(1, 128 // 4) + 1, jnp.int32)
        fside_S2_0 = -0.00337071 + 1.01897 * jax.random.normal(jax.random.fold_in(_rk, 11), (128,), jnp.float32)
        _ctx_2048P = jax.random.normal(jax.random.fold_in(_rk, 12), (8, 16, 256), jnp.float32)
        _ctx_2048c = jax.random.dirichlet(jax.random.fold_in(_rk, 512), 0.3 * jnp.ones((16,), jnp.float32), (8, 128))
        _ctx_2048t = jnp.einsum('bsk,bkd->bsd', _ctx_2048c, _ctx_2048P)
        _ctx_2048t = _ctx_2048t * jax.lax.rsqrt(jnp.mean(jnp.square(_ctx_2048t)) + 1e-12) * 0.953939
        ctx_2048 = 0.000675642 + 1.00031 * (_ctx_2048t + 0.3 * jax.random.normal(jax.random.fold_in(_rk, 612), (8, 128, 256), jnp.float32))
        _validS = jnp.arange(128)[None, :] < _lenS[:, None]
        _validS2 = jnp.arange(128)[None, :] < _lenS2[:, None]
        _causal = jnp.tril(jnp.ones((128, 128), dtype=bool))
        mask_SxS2_bc0 = jnp.logical_not(jnp.broadcast_to(_validS2[0:1, :], (128, 128)))
        mask_BxS2_bk0 = jnp.logical_not(jnp.broadcast_to(_validS2[:, :], (8, 128)))
        return (x, fside_S2_0, ctx_2048, mask_SxS2_bc0, mask_BxS2_bk0)
    x, fside_S2_0, ctx_2048, mask_SxS2_bc0, mask_BxS2_bk0 = _rec_inputs()

    def _L0_attn_setup():
        import jax, jax.numpy as jnp
        import numpy as np
        import math
        D_MODEL = 256
        N_HEADS = 16
        D_HEAD = D_MODEL // N_HEADS
        key = jax.random.key(seed)
        ks = jax.random.split(key, 6)
        B, S, D = (4, 256, D_MODEL)
        scale = 1.0 / math.sqrt(D)
        x = jax.random.normal(ks[0], (B, S, D), dtype=jnp.float32)
        Wq = jax.random.normal(ks[1], (D, D), dtype=jnp.float32) * scale
        Wk = jax.random.normal(ks[2], (D, D), dtype=jnp.float32) * scale
        Wv = jax.random.normal(ks[3], (D, D), dtype=jnp.float32) * scale
        Wo = jax.random.normal(ks[4], (D, D), dtype=jnp.float32) * scale
        bo = jax.random.normal(ks[5], (D,), dtype=jnp.float32) * 0.01
        return {'x': x, 'Wq': Wq, 'Wk': Wk, 'Wv': Wv, 'Wo': Wo, 'bo': bo}
    _L0_attn_all = _L0_attn_setup()
    _L0_attn_in = {k: v for k, v in _L0_attn_all.items() if k in ('Wq', 'Wk', 'Wv', 'Wo', 'bo')}
    del _L0_attn_all

    def _L0_xattn_setup():
        import jax, jax.numpy as jnp
        import numpy as np
        key = jax.random.key(seed)
        ks = jax.random.split(key, 5)
        B, D, L, NH = (2, 128, 256, 8)
        H = D // NH
        return {'v': jax.random.normal(ks[0], (B, D, L), jnp.float32), 'k': jax.random.normal(ks[1], (H, L), jnp.float32) * 0.1, 'bias': jax.random.normal(ks[2], (D,), jnp.float32), 'x1': jax.random.normal(ks[3], (B, D, L), jnp.float32), 'x2': jax.random.normal(ks[4], (B, D, L), jnp.float32), 'num_heads': NH}
    _L0_xattn_all = _L0_xattn_setup()
    _L0_xattn_in = {k: v for k, v in _L0_xattn_all.items() if k in ('k',)}
    del _L0_xattn_all

    def _L0_ffn_setup():
        import jax, jax.numpy as jnp
        import numpy as np
        D_MODEL, D_FF, NS, NR, KR = (256, 176, 2, 16, 4)
        B, S = (4, 256)

        def _moe_forward(u, shared_w1, shared_b1, shared_w2, shared_b2, routed_w1, routed_b1, routed_w2, routed_b2, centroids, bias):
            b, s, d = u.shape
            flat = u.reshape(-1, d)
            T = flat.shape[0]
            h = jax.nn.relu(jnp.einsum('td,ndf->ntf', flat, shared_w1) + shared_b1[:, None, :])
            shared_out = jnp.einsum('ntf,nfd->td', h, shared_w2) + shared_b2.sum(0)
            out = flat + shared_out
            scores = jax.nn.sigmoid(flat @ centroids.T) + bias
            vals, idx = jax.lax.top_k(scores, KR)
            gating = jnp.zeros_like(scores).at[jnp.arange(T)[:, None], idx].set(vals)
            gating = gating / jnp.clip(gating.sum(-1, keepdims=True), 1e-08)

            def step(acc, ew):
                w1, b1, w2, b2, g = ew
                hj = jax.nn.relu(flat @ w1 + b1)
                yj = hj @ w2 + b2
                return (acc + yj * g[:, None], None)
            rout0 = jnp.zeros_like(flat)
            rout, _ = jax.lax.scan(step, rout0, (routed_w1, routed_b1, routed_w2, routed_b2, gating.T))
            return (out + rout).reshape(b, s, d)
        key = jax.random.key(seed)
        ks = jax.random.split(key, 10)
        s1 = 1.0 / np.sqrt(D_MODEL)
        s2 = 1.0 / np.sqrt(D_FF)
        return {'u': jax.random.normal(ks[0], (B, S, D_MODEL), dtype=jnp.float32), 'shared_w1': jax.random.normal(ks[1], (NS, D_MODEL, D_FF), dtype=jnp.float32) * s1, 'shared_b1': jnp.zeros((NS, D_FF), dtype=jnp.float32), 'shared_w2': jax.random.normal(ks[2], (NS, D_FF, D_MODEL), dtype=jnp.float32) * s2, 'shared_b2': jnp.zeros((NS, D_MODEL), dtype=jnp.float32), 'routed_w1': jax.random.normal(ks[3], (NR, D_MODEL, D_FF), dtype=jnp.float32) * s1, 'routed_b1': jnp.zeros((NR, D_FF), dtype=jnp.float32), 'routed_w2': jax.random.normal(ks[4], (NR, D_FF, D_MODEL), dtype=jnp.float32) * s2, 'routed_b2': jnp.zeros((NR, D_MODEL), dtype=jnp.float32), 'centroids': jax.random.normal(ks[5], (NR, D_MODEL), dtype=jnp.float32) * s1, 'bias': jnp.zeros((NR,), dtype=jnp.float32)}
    _L0_ffn_all = _L0_ffn_setup()
    _L0_ffn_in = {k: v for k, v in _L0_ffn_all.items() if k in ('shared_w1', 'shared_b1', 'shared_w2', 'shared_b2', 'routed_w1', 'routed_b1', 'routed_w2', 'routed_b2', 'centroids', 'bias')}
    del _L0_ffn_all

    def _L1_attn_setup():
        import jax, jax.numpy as jnp
        import numpy as np
        N_HEADS = 16
        key = jax.random.key(seed)
        ks = jax.random.split(key, 9)
        B, S, D = (2, 256, 256)
        s = 0.02
        return {'X': jax.random.normal(ks[0], (B, S, D), jnp.float32), 'Wq': jax.random.normal(ks[1], (D, D), jnp.float32) * s, 'bq': jax.random.normal(ks[2], (D,), jnp.float32) * s, 'Wk': jax.random.normal(ks[3], (D, D), jnp.float32) * s, 'bk': jax.random.normal(ks[4], (D,), jnp.float32) * s, 'Wv': jax.random.normal(ks[5], (D, D), jnp.float32) * s, 'bv': jax.random.normal(ks[6], (D,), jnp.float32) * s, 'Wo': jax.random.normal(ks[7], (D, D), jnp.float32) * s, 'bo': jax.random.normal(ks[8], (D,), jnp.float32) * s}
    _L1_attn_all = _L1_attn_setup()
    _L1_attn_in = {k: v for k, v in _L1_attn_all.items() if k in ('Wq', 'bq', 'Wk', 'bk', 'Wv', 'bv', 'Wo', 'bo')}
    del _L1_attn_all

    def _L1_xattn_setup():
        import jax, jax.numpy as jnp
        import numpy as np
        B, LQ, LKV = (4, 128, 128)
        HID, H, G = (256, 32, 8)
        HD = HID // H
        HPG = H // G
        key = jax.random.key(seed)
        ks = jax.random.split(key, 10)
        s = 0.02
        inp = {'X': jax.random.normal(ks[0], (B, LQ, HID), jnp.float32), 'encoder_output': jax.random.normal(ks[1], (B, LKV, HID), jnp.float32), 'causal_mask': jnp.triu(jnp.ones((LQ, LKV), bool), 1), 'padding_mask': jnp.zeros((B, LKV), bool).at[B // 2:, LKV - LKV // 4:].set(True), 'Wq': jax.random.normal(ks[2], (HID, HID), jnp.float32) * s, 'bq': jnp.zeros((HID,), jnp.float32), 'Wk': jax.random.normal(ks[3], (G * HD, HID), jnp.float32) * s, 'bk': jnp.zeros((G * HD,), jnp.float32), 'Wv': jax.random.normal(ks[4], (G * HD, HID), jnp.float32) * s, 'bv': jnp.zeros((G * HD,), jnp.float32), 'Wo': jax.random.normal(ks[5], (HID, HID), jnp.float32) * s, 'bo': jnp.zeros((HID,), jnp.float32)}
        return inp
    _L1_xattn_all = _L1_xattn_setup()
    _L1_xattn_in = {k: v for k, v in _L1_xattn_all.items() if k in ('Wq', 'bq', 'Wk', 'bk', 'Wv', 'bv', 'Wo', 'bo')}
    del _L1_xattn_all

    def _L1_ffn_setup():
        import math
        import jax, jax.numpy as jnp
        import numpy as np
        from jax import lax
        D = 256
        I = 128
        E = 32
        K = 4
        NG = 8
        TKG = 3
        NSH = 2
        SCALE = 2.5
        CF = 1.25
        B, S = (2, 256)

        def _router(x, router_w, e_bias):
            scores = jax.nn.sigmoid(x @ router_w.T)
            sc = scores + e_bias[None, :]
            T = x.shape[0]
            gs = sc.reshape(T, NG, E // NG)
            group_scores = lax.top_k(gs, 2)[0].sum(-1)
            _, gidx = lax.top_k(group_scores, TKG)
            gmask = jnp.zeros((T, NG), sc.dtype).at[jnp.arange(T)[:, None], gidx].set(1.0)
            smask = jnp.repeat(gmask, E // NG, axis=1)
            masked = jnp.where(smask > 0, sc, 0.0)
            _, topk_idx = lax.top_k(masked, K)
            topk_w = jnp.take_along_axis(scores, topk_idx, axis=1)
            topk_w = topk_w / (topk_w.sum(-1, keepdims=True) + 1e-20)
            topk_w = topk_w * SCALE
            return (topk_idx.astype(jnp.int32), topk_w)

        def _moe_forward(hidden_states, router_w, e_bias, W_gate, W_up, W_down, shared_gate, shared_up, shared_down):
            b, s, d = hidden_states.shape
            T = b * s
            C = int(math.ceil(CF * T / E))
            EC = E * C
            x = hidden_states.reshape(T, d)
            topk_idx, topk_w = _router(x, router_w, e_bias)
            expert_flat = topk_idx.reshape(-1)
            w_flat = topk_w.reshape(-1)
            tok_flat = jnp.repeat(jnp.arange(T, dtype=jnp.int32), K)
            sort_ix = jnp.argsort(expert_flat)
            e_sorted = expert_flat[sort_ix]
            tok_s = tok_flat[sort_ix]
            w_s = w_flat[sort_ix]
            counts = jnp.zeros(E, jnp.int32).at[e_sorted].add(1)
            group_start = jnp.concatenate([jnp.zeros(1, jnp.int32), jnp.cumsum(counts)[:-1].astype(jnp.int32)])
            pos = jnp.arange(T * K, dtype=jnp.int32) - group_start[e_sorted]
            valid = pos < C
            dest = e_sorted * C + jnp.where(valid, pos, 0)
            slots_token = jnp.zeros(EC, jnp.int32).at[dest].add(jnp.where(valid, tok_s, 0))
            slots_w = jnp.zeros(EC, w_s.dtype).at[dest].add(jnp.where(valid, w_s, 0.0))
            Xp = x[slots_token].reshape(E, C, d)
            G = jnp.einsum('ecd,edi->eci', Xp, W_gate)
            U = jnp.einsum('ecd,edi->eci', Xp, W_up)
            Y = jnp.einsum('eci,eid->ecd', jax.nn.silu(G) * U, W_down)
            Yf = Y.reshape(EC, d) * slots_w[:, None]
            out = jnp.zeros((T, d), x.dtype).at[slots_token].add(Yf)
            shared = jax.nn.silu(x @ shared_gate.T) * (x @ shared_up.T) @ shared_down.T
            return (out + shared).reshape(b, s, d)
        key = jax.random.key(seed)
        ks = jax.random.split(key, 8)

        def rn(k, shape, scale=0.02):
            return jax.random.normal(k, shape, jnp.float32) * scale
        return {'hidden_states': jax.random.normal(ks[0], (B, S, D), jnp.float32), 'router_w': rn(ks[1], (E, D)), 'e_bias': jnp.zeros((E,), jnp.float32), 'W_gate': rn(ks[2], (E, D, I)), 'W_up': rn(ks[3], (E, D, I)), 'W_down': rn(ks[4], (E, I, D)), 'shared_gate': rn(ks[5], (I * NSH, D)), 'shared_up': rn(ks[6], (I * NSH, D)), 'shared_down': rn(ks[7], (D, I * NSH))}
    _L1_ffn_all = _L1_ffn_setup()
    _L1_ffn_in = {k: v for k, v in _L1_ffn_all.items() if k in ('router_w', 'e_bias', 'W_gate', 'W_up', 'W_down', 'shared_gate', 'shared_up', 'shared_down')}
    del _L1_ffn_all
    return {'x': x, 'fside_S2_0': fside_S2_0, 'ctx_2048': ctx_2048, 'mask_SxS2_bc0': mask_SxS2_bc0, 'mask_BxS2_bk0': mask_BxS2_bk0, 'L0_attn_Wq': _L0_attn_in['Wq'], 'L0_attn_Wk': _L0_attn_in['Wk'], 'L0_attn_Wv': _L0_attn_in['Wv'], 'L0_attn_Wo': _L0_attn_in['Wo'], 'L0_attn_bo': _L0_attn_in['bo'], 'L0_xattn_k': _L0_xattn_in['k'], 'L0_ffn_shared_w1': _L0_ffn_in['shared_w1'], 'L0_ffn_shared_b1': _L0_ffn_in['shared_b1'], 'L0_ffn_shared_w2': _L0_ffn_in['shared_w2'], 'L0_ffn_shared_b2': _L0_ffn_in['shared_b2'], 'L0_ffn_routed_w1': _L0_ffn_in['routed_w1'], 'L0_ffn_routed_b1': _L0_ffn_in['routed_b1'], 'L0_ffn_routed_w2': _L0_ffn_in['routed_w2'], 'L0_ffn_routed_b2': _L0_ffn_in['routed_b2'], 'L0_ffn_centroids': _L0_ffn_in['centroids'], 'L0_ffn_bias': _L0_ffn_in['bias'], 'L1_attn_Wq': _L1_attn_in['Wq'], 'L1_attn_bq': _L1_attn_in['bq'], 'L1_attn_Wk': _L1_attn_in['Wk'], 'L1_attn_bk': _L1_attn_in['bk'], 'L1_attn_Wv': _L1_attn_in['Wv'], 'L1_attn_bv': _L1_attn_in['bv'], 'L1_attn_Wo': _L1_attn_in['Wo'], 'L1_attn_bo': _L1_attn_in['bo'], 'L1_xattn_Wq': _L1_xattn_in['Wq'], 'L1_xattn_bq': _L1_xattn_in['bq'], 'L1_xattn_Wk': _L1_xattn_in['Wk'], 'L1_xattn_bk': _L1_xattn_in['bk'], 'L1_xattn_Wv': _L1_xattn_in['Wv'], 'L1_xattn_bv': _L1_xattn_in['bv'], 'L1_xattn_Wo': _L1_xattn_in['Wo'], 'L1_xattn_bo': _L1_xattn_in['bo'], 'L1_ffn_router_w': _L1_ffn_in['router_w'], 'L1_ffn_e_bias': _L1_ffn_in['e_bias'], 'L1_ffn_W_gate': _L1_ffn_in['W_gate'], 'L1_ffn_W_up': _L1_ffn_in['W_up'], 'L1_ffn_W_down': _L1_ffn_in['W_down'], 'L1_ffn_shared_gate': _L1_ffn_in['shared_gate'], 'L1_ffn_shared_up': _L1_ffn_in['shared_up'], 'L1_ffn_shared_down': _L1_ffn_in['shared_down']}

def reference(x, fside_S2_0, ctx_2048, mask_SxS2_bc0, mask_BxS2_bk0, L0_attn_Wq, L0_attn_Wk, L0_attn_Wv, L0_attn_Wo, L0_attn_bo, L0_xattn_k, L0_ffn_shared_w1, L0_ffn_shared_b1, L0_ffn_shared_w2, L0_ffn_shared_b2, L0_ffn_routed_w1, L0_ffn_routed_b1, L0_ffn_routed_w2, L0_ffn_routed_b2, L0_ffn_centroids, L0_ffn_bias, L1_attn_Wq, L1_attn_bq, L1_attn_Wk, L1_attn_bk, L1_attn_Wv, L1_attn_bv, L1_attn_Wo, L1_attn_bo, L1_xattn_Wq, L1_xattn_bq, L1_xattn_Wk, L1_xattn_bk, L1_xattn_Wv, L1_xattn_bv, L1_xattn_Wo, L1_xattn_bo, L1_ffn_router_w, L1_ffn_e_bias, L1_ffn_W_gate, L1_ffn_W_up, L1_ffn_W_down, L1_ffn_shared_gate, L1_ffn_shared_up, L1_ffn_shared_down):
    import jax
    import jax.numpy as jnp

    def _L0_attn_ref(x, Wq, Wk, Wv, Wo, bo):
        import jax, jax.numpy as jnp
        import numpy as np
        import math
        D_MODEL = 256
        N_HEADS = 16
        D_HEAD = D_MODEL // N_HEADS
        B, S, D = x.shape
        H, Dh = (N_HEADS, D_HEAD)
        q = (x @ Wq.T).reshape(B, S, H, Dh).transpose(0, 2, 1, 3)
        k = (x @ Wk.T).reshape(B, S, H, Dh).transpose(0, 2, 1, 3)
        v = (x @ Wv.T).reshape(B, S, H, Dh).transpose(0, 2, 1, 3)
        scores = jnp.einsum('bhqd,bhkd->bhqk', q, k) / math.sqrt(Dh)
        causal = jnp.tril(jnp.ones((S, S), dtype=bool))
        scores = jnp.where(causal, scores, -jnp.inf)
        attn = jax.nn.softmax(scores, axis=-1)
        out = jnp.einsum('bhqk,bhkd->bhqd', attn, v)
        out = out.transpose(0, 2, 1, 3).reshape(B, S, D)
        return out @ Wo.T + bo

    def _L0_xattn_ref(v, k, bias, x1, x2, num_heads):
        import jax, jax.numpy as jnp
        import numpy as np
        B, D, L = v.shape
        H = D // num_heads
        fft_size = 2 * L
        vr = v.reshape(B, H, num_heads, L)
        x1r = x1.reshape(B, H, num_heads, L)
        x2r = x2.reshape(B, H, num_heads, L)
        kv = vr[:, :, :, None, :] * x2r[:, :, None, :, :]
        k_f = jnp.fft.rfft(k.astype(jnp.float32), n=fft_size)
        y = jnp.fft.irfft(jnp.fft.rfft(kv, n=fft_size) * k_f[None, :, None, None, :], n=fft_size)[..., :L]
        skip = bias.astype(jnp.float32).reshape(H, num_heads)[None, :, :, None, None]
        y = y + kv * skip
        out = jnp.einsum('bhijl,bhil->bhjl', y, x1r)
        return out.reshape(B, D, L)

    def _L0_ffn_ref(u, shared_w1, shared_b1, shared_w2, shared_b2, routed_w1, routed_b1, routed_w2, routed_b2, centroids, bias):
        import jax, jax.numpy as jnp
        import numpy as np
        D_MODEL, D_FF, NS, NR, KR = (256, 176, 2, 16, 4)
        B, S = (4, 256)

        def _moe_forward(u, shared_w1, shared_b1, shared_w2, shared_b2, routed_w1, routed_b1, routed_w2, routed_b2, centroids, bias):
            b, s, d = u.shape
            flat = u.reshape(-1, d)
            T = flat.shape[0]
            h = jax.nn.relu(jnp.einsum('td,ndf->ntf', flat, shared_w1) + shared_b1[:, None, :])
            shared_out = jnp.einsum('ntf,nfd->td', h, shared_w2) + shared_b2.sum(0)
            out = flat + shared_out
            scores = jax.nn.sigmoid(flat @ centroids.T) + bias
            vals, idx = jax.lax.top_k(scores, KR)
            gating = jnp.zeros_like(scores).at[jnp.arange(T)[:, None], idx].set(vals)
            gating = gating / jnp.clip(gating.sum(-1, keepdims=True), 1e-08)

            def step(acc, ew):
                w1, b1, w2, b2, g = ew
                hj = jax.nn.relu(flat @ w1 + b1)
                yj = hj @ w2 + b2
                return (acc + yj * g[:, None], None)
            rout0 = jnp.zeros_like(flat)
            rout, _ = jax.lax.scan(step, rout0, (routed_w1, routed_b1, routed_w2, routed_b2, gating.T))
            return (out + rout).reshape(b, s, d)
        return _moe_forward(u, shared_w1, shared_b1, shared_w2, shared_b2, routed_w1, routed_b1, routed_w2, routed_b2, centroids, bias)

    def _L1_attn_ref(X, Wq, bq, Wk, bk, Wv, bv, Wo, bo):
        import jax, jax.numpy as jnp
        import numpy as np
        N_HEADS = 16
        B, S, D = X.shape
        H = N_HEADS
        d_head = D // H
        scale = jnp.asarray(1.0 / np.sqrt(np.sqrt(d_head)), X.dtype)
        Q = (X @ Wq.T + bq).reshape(B, S, H, d_head) * scale
        K = (X @ Wk.T + bk).reshape(B, S, H, d_head) * scale
        V = (X @ Wv.T + bv).reshape(B, S, H, d_head)
        scores = jnp.einsum('bqhd,bkhd->bhqk', Q, K)
        causal = jnp.tril(jnp.ones((S, S), bool))
        scores = jnp.where(causal[None, None], scores, -jnp.inf)
        attn = jax.nn.softmax(scores.astype(jnp.float32), axis=-1).astype(X.dtype)
        out = jnp.einsum('bhqk,bkhd->bqhd', attn, V).reshape(B, S, D)
        return out @ Wo.T + bo

    def _L1_xattn_ref(X, encoder_output, causal_mask, padding_mask, Wq, bq, Wk, bk, Wv, bv, Wo, bo):
        import jax, jax.numpy as jnp
        import numpy as np
        B, LQ, LKV = (4, 128, 128)
        HID, H, G = (256, 32, 8)
        HD = HID // H
        HPG = H // G
        b = X.shape[0]
        q = X @ Wq.T + bq
        k = encoder_output @ Wk.T + bk
        v = encoder_output @ Wv.T + bv
        q = q.reshape(b, LQ, G, HPG, HD).transpose(0, 2, 3, 1, 4)
        k = k.reshape(b, LKV, G, HD).transpose(0, 2, 1, 3)
        v = v.reshape(b, LKV, G, HD).transpose(0, 2, 1, 3)
        scores = jnp.einsum('bgrqd,bgkd->bgrqk', q, k) / jnp.sqrt(jnp.float32(HD))
        scores = jnp.where(causal_mask[None, None, None, :, :], -jnp.inf, scores)
        scores = jnp.where(padding_mask[:, None, None, None, :], -jnp.inf, scores)
        w = jax.nn.softmax(scores, axis=-1)
        out = jnp.einsum('bgrqk,bgkd->bgrqd', w, v)
        out = out.reshape(b, H, LQ, HD).transpose(0, 2, 1, 3).reshape(b, LQ, HID)
        return out @ Wo.T + bo

    def _L1_ffn_ref(hidden_states, router_w, e_bias, W_gate, W_up, W_down, shared_gate, shared_up, shared_down):
        import math
        import jax, jax.numpy as jnp
        import numpy as np
        from jax import lax
        D = 256
        I = 128
        E = 32
        K = 4
        NG = 8
        TKG = 3
        NSH = 2
        SCALE = 2.5
        CF = 1.25
        B, S = (2, 256)

        def _router(x, router_w, e_bias):
            scores = jax.nn.sigmoid(x @ router_w.T)
            sc = scores + e_bias[None, :]
            T = x.shape[0]
            gs = sc.reshape(T, NG, E // NG)
            group_scores = lax.top_k(gs, 2)[0].sum(-1)
            _, gidx = lax.top_k(group_scores, TKG)
            gmask = jnp.zeros((T, NG), sc.dtype).at[jnp.arange(T)[:, None], gidx].set(1.0)
            smask = jnp.repeat(gmask, E // NG, axis=1)
            masked = jnp.where(smask > 0, sc, 0.0)
            _, topk_idx = lax.top_k(masked, K)
            topk_w = jnp.take_along_axis(scores, topk_idx, axis=1)
            topk_w = topk_w / (topk_w.sum(-1, keepdims=True) + 1e-20)
            topk_w = topk_w * SCALE
            return (topk_idx.astype(jnp.int32), topk_w)

        def _moe_forward(hidden_states, router_w, e_bias, W_gate, W_up, W_down, shared_gate, shared_up, shared_down):
            b, s, d = hidden_states.shape
            T = b * s
            C = int(math.ceil(CF * T / E))
            EC = E * C
            x = hidden_states.reshape(T, d)
            topk_idx, topk_w = _router(x, router_w, e_bias)
            expert_flat = topk_idx.reshape(-1)
            w_flat = topk_w.reshape(-1)
            tok_flat = jnp.repeat(jnp.arange(T, dtype=jnp.int32), K)
            sort_ix = jnp.argsort(expert_flat)
            e_sorted = expert_flat[sort_ix]
            tok_s = tok_flat[sort_ix]
            w_s = w_flat[sort_ix]
            counts = jnp.zeros(E, jnp.int32).at[e_sorted].add(1)
            group_start = jnp.concatenate([jnp.zeros(1, jnp.int32), jnp.cumsum(counts)[:-1].astype(jnp.int32)])
            pos = jnp.arange(T * K, dtype=jnp.int32) - group_start[e_sorted]
            valid = pos < C
            dest = e_sorted * C + jnp.where(valid, pos, 0)
            slots_token = jnp.zeros(EC, jnp.int32).at[dest].add(jnp.where(valid, tok_s, 0))
            slots_w = jnp.zeros(EC, w_s.dtype).at[dest].add(jnp.where(valid, w_s, 0.0))
            Xp = x[slots_token].reshape(E, C, d)
            G = jnp.einsum('ecd,edi->eci', Xp, W_gate)
            U = jnp.einsum('ecd,edi->eci', Xp, W_up)
            Y = jnp.einsum('eci,eid->ecd', jax.nn.silu(G) * U, W_down)
            Yf = Y.reshape(EC, d) * slots_w[:, None]
            out = jnp.zeros((T, d), x.dtype).at[slots_token].add(Yf)
            shared = jax.nn.silu(x @ shared_gate.T) * (x @ shared_up.T) @ shared_down.T
            return (out + shared).reshape(b, s, d)
        return _moe_forward(hidden_states, router_w, e_bias, W_gate, W_up, W_down, shared_gate, shared_up, shared_down)
    x = x + _L0_attn_ref(_layernorm(x, axis=-1), L0_attn_Wq, L0_attn_Wk, L0_attn_Wv, L0_attn_Wo, L0_attn_bo)
    x = x + _L0_xattn_ref(_layernorm(x, axis=-1), L0_xattn_k, fside_S2_0, ctx_2048, ctx_2048, 8)
    x = x + _L0_ffn_ref(_layernorm(x, axis=-1), L0_ffn_shared_w1, L0_ffn_shared_b1, L0_ffn_shared_w2, L0_ffn_shared_b2, L0_ffn_routed_w1, L0_ffn_routed_b1, L0_ffn_routed_w2, L0_ffn_routed_b2, L0_ffn_centroids, L0_ffn_bias)
    x = x + _L1_attn_ref(_layernorm(x, axis=-1), L1_attn_Wq, L1_attn_bq, L1_attn_Wk, L1_attn_bk, L1_attn_Wv, L1_attn_bv, L1_attn_Wo, L1_attn_bo)
    x = x + _L1_xattn_ref(_layernorm(x, axis=-1), ctx_2048, mask_SxS2_bc0, mask_BxS2_bk0, L1_xattn_Wq, L1_xattn_bq, L1_xattn_Wk, L1_xattn_bk, L1_xattn_Wv, L1_xattn_bv, L1_xattn_Wo, L1_xattn_bo)
    x = x + _L1_ffn_ref(_layernorm(x, axis=-1), L1_ffn_router_w, L1_ffn_e_bias, L1_ffn_W_gate, L1_ffn_W_up, L1_ffn_W_down, L1_ffn_shared_gate, L1_ffn_shared_up, L1_ffn_shared_down)
    return x

_drawn_inputs = setup_inputs


def setup_inputs(seed=0):
    import zlib

    import numpy as np

    out = dict(_drawn_inputs(seed))
    spreads = {'L0_ffn_shared_b1': (0.0, 0.507),
     'L0_ffn_shared_b2': (0.0, 0.348),
     'L0_ffn_routed_b1': (0.0, 0.8),
     'L0_ffn_routed_b2': (0.0, 0.8),
     'L0_ffn_bias': (0.0, 0.1),
     'L1_xattn_bq': (0.0, 0.8),
     'L1_xattn_bk': (0.0, 0.8),
     'L1_xattn_bv': (0.0, 0.8),
     'L1_xattn_bo': (0.0, 0.494),
     'L1_ffn_e_bias': (0.0, 0.8)}
    factors = {'L0_attn_bo': 3.851,
     'L1_attn_Wq': 8.0,
     'L1_attn_bq': 8.0,
     'L1_attn_Wk': 8.0,
     'L1_attn_bk': 8.0,
     'L1_attn_Wv': 8.0,
     'L1_attn_bv': 8.0,
     'L1_attn_Wo': 8.0,
     'L1_attn_bo': 8.0,
     'L1_xattn_Wq': 8.0,
     'L1_xattn_Wk': 8.0,
     'L1_xattn_Wv': 6.486,
     'L1_xattn_Wo': 5.845,
     'L1_ffn_router_w': 8.0,
     'L1_ffn_W_gate': 8.0,
     'L1_ffn_W_up': 8.0,
     'L1_ffn_W_down': 8.0,
     'L1_ffn_shared_gate': 8.0,
     'L1_ffn_shared_up': 8.0,
     'L1_ffn_shared_down': 8.0}
    for name, (base, spread) in spreads.items():
        noise = np.random.default_rng([zlib.crc32(name.encode()), seed]).standard_normal(out[name].shape)
        drawn = base * np.exp(spread * noise) if base else spread * noise
        out[name] = jnp.asarray(drawn.astype(out[name].dtype))
    for name, factor in factors.items():
        out[name] = (out[name] * factor).astype(out[name].dtype)
    return out
```

```python
from contextlib import ExitStack

import concourse.bass as bass
from concourse import mybir
from concourse.alu_op_type import AluOpType as ALU

ACT = mybir.ActivationFunctionType
AX = mybir.AxisListType
F32 = mybir.dt.float32
BF16 = mybir.dt.bfloat16
F16 = mybir.dt.float16
U8 = mybir.dt.uint8

P = 128
B = 8
D = 256
DC = D // P
T = B * P
EPS = 1e-5
NEG = -1.0e30
FAR = -3.0e38
HF = 512
NH = T // HF

CH, CI = 16, 8

NS, NR, FF, KR = 2, 16, 176, 4
NE0 = NS + NR
F0 = NE0 * FF
NB0 = -(-F0 // P)
LAST0 = F0 - (NB0 - 1) * P
GROUP = 32

E1, I1, NG1, TKG, K1 = 32, 128, 8, 3, 4
CAP = -(-5 * T // (4 * E1))
SLOTS = E1 * CAP
SC = SLOTS // P
SCALE1 = 2.5
ESPAN = [(0, 11), (11, 22), (22, 32)]
WRING = 16


def decoder_kernel(nc, A, out, stages=6):
    ctx = ExitStack()
    with ctx:
        def sb(name, shape, dt=F32):
            return ctx.enter_context(nc.sbuf_tensor(name, shape, dt))

        sems = {}

        def S(name):
            if name not in sems:
                sems[name] = ctx.enter_context(nc.semaphore(name))
            return sems[name]

        X = sb("X", [P, B, D])
        xn = sb("xn", [P, B, D])
        xnT = sb("xnT", [P, DC, T])
        CT = sb("CT", [P, B, D])
        ctxT = sb("ctxT", [P, DC, T])
        wraw = [sb(f"wraw{i}", [P, 4, DC, D]) for i in range(2)]
        WT = sb("WT", [P, 4, DC, D])
        ident = sb("ident", [P, P])
        identb = sb("identb", [P, P], BF16)
        identh = sb("identh", [P, P], F16)
        causal = sb("causal", [P, P], BF16)
        chgroup = sb("chgroup", [P, P])
        before = sb("before", [P, P], BF16)
        onesb = sb("onesb", [P, P], BF16)
        slot_iota = sb("slot_iota", [P, CAP])
        skip = sb("skip", [P, 1])
        bcol = sb("bcol", [P, 3, 4])
        bbc = sb("bbc", [P, 5, D])
        bias0 = sb("bias0", [P, NR])
        ebias = sb("ebias", [P, E1])
        stats = sb("stats", [P, B, 6])
        mv = sb("mv", [P, B, 2])
        rstd = sb("rstd", [P, B])
        veps = sb("veps", [P, B])
        mhalf = sb("mhalf", [P, 1])
        mx = sb("mx", [P, 2, 8])
        rec = sb("rec", [P, 2, 32])
        cen_raw = sb("cen_raw", [NR, D])
        cenT = sb("cenT", [P, DC, NR])
        rw_raw = sb("rw_raw", [E1, D])
        rwT = sb("rwT", [P, DC, E1])
        b1row = sb("b1row", [NB0, P])
        b1col = sb("b1col", [P, NB0])
        b2cat = sb("b2cat", [NE0, D])

        R1 = sb("R1", [P, DC * F0 + NB0 * D])
        W1 = R1[:, 0:DC * F0].rearrange("p (c f) -> p c f", c=DC)
        W2 = R1[:, DC * F0:DC * F0 + NB0 * D].rearrange("p (k d) -> p k d", k=NB0)
        EW = R1[:, 0:WRING * 3 * D].rearrange("p (e w) -> p e w", e=WRING)

        R2 = sb("R2", [P, 16384])
        pair = R2[:, 0:4096].bitcast(F16).rearrange("p (s c t) -> p s c t", s=4, c=DC)
        Ph = R2[:, 0:2048].bitcast(F16).rearrange("p (n h k) -> p n h k", n=4, h=8)
        Pl = R2[:, 2048:4096].bitcast(F16).rearrange("p (n h k) -> p n h k", n=4, h=8)
        QS = R2[:, 4096:8192].bitcast(F16).rearrange("p (g t) -> p g t", g=8)
        KSa = R1[:, 4096:8192].bitcast(F16).rearrange("p (g t) -> p g t", g=8)
        KSb = R2[:, 8192:12288].bitcast(F16).rearrange("p (g t) -> p g t", g=8)
        VH = R2[:, 12288:13376].bitcast(F16)
        VL = R2[:, 13376:14464].bitcast(F16)
        V16 = [v_.rearrange("p (b h e) -> p b h e", b=B, h=16) for v_ in (VH, VL)]
        V8 = [v_[:, 0:B * 72].rearrange("p (b h e) -> p b h e", b=B, h=8) for v_ in (VH, VL)]
        Toe = R2[:, 8192:12288].rearrange("p (h l) -> p h l", h=CH)
        xmask = R2[:, 14464:14464 + B * P // 2].bitcast(BF16).rearrange("p (b k) -> p b k", b=B)
        att = R2[:, 14976:14976 + 2 * D].rearrange("p (n d) -> p n d", n=2)
        vf = att
        attT = R2[:, 15488:15488 + D].rearrange("p (c t) -> p c t", c=DC)
        mk8 = R2[:, 15744:16000].bitcast(U8).rearrange("p (b k) -> p b k", b=B)
        mq8 = R2[:, 16000:16032].bitcast(U8)
        kv = R2[:, 0:2048].rearrange("p (n c t) -> p n c t", n=2, c=DC)
        kin = R1[0:CH, 0:D]
        krev = R1[0:CH, D:2 * D + P]
        zb = R2[:, 2048:4096].rearrange("p (n t) -> p n t", n=4)
        oT = R2[:, 4096:6144].rearrange("p (c t) -> p c t", c=DC)
        ub = R2[:, 6144:8192].rearrange("p (b d) -> p b d", b=B)
        wb = R2[:, 12288:14336].rearrange("p (b d) -> p b d", b=B)
        hid = R2[:, 0:1024].rearrange("p (n t) -> p n t", n=2)
        hg = R2[:, 1024:2048].rearrange("p (n t) -> p n t", n=2)
        sel = wraw[0][:, :, :, :].rearrange("p a c d -> p (a c d)")[:, 0:F0 // 2].bitcast(BF16)
        g0T = R2[0:NE0, 6800:6800 + T]
        g3T = R2[:, 3700:3700 + T // 2].bitcast(BF16)
        o = 4400
        sc0 = R2[:, o:o + B * 20].rearrange("p (b e) -> p b e", b=B)
        rp0 = R2[:, o + 160:o + 320].rearrange("p (b e) -> p b e", b=B)
        m80 = R2[:, o + 320:o + 384].rearrange("p (b e) -> p b e", b=B)
        gv0 = R2[:, o + 384:o + 512].rearrange("p (b e) -> p b e", b=B)
        gs0 = R2[:, o + 512:o + 520]
        gr0 = R2[:, o + 520:o + 528]
        G3 = R2[:, o + 528:o + 528 + B * 96].rearrange("p (b e) -> p b e", b=B)
        gb0 = R2[:, o + 1296:o + 1296 + B * 8].bitcast(BF16).rearrange("p (b e) -> p b e", b=B)
        gf0 = R2[:, o + 1400:o + 1400 + B * NE0].rearrange("p (b e) -> p b e", b=B)
        rs0 = R2[:, o + 1600:o + 1600 + B * 16].rearrange("p (b e) -> p b e", b=B)
        Pm = R2[:, 0:B * SLOTS // 2].bitcast(BF16).rearrange("p (b s) -> p b s", b=B)
        PmT = R2[:, 5120:5120 + SC * T // 2].bitcast(BF16).rearrange("p (k t) -> p k t", k=SC)
        XpT = R2[:, 10240:10240 + 2 * SLOTS].rearrange("p (c s) -> p c s", c=DC)
        yT = R2[:, 12800:12800 + 2 * SLOTS].rearrange("p (c s) -> p c s", c=DC)
        Y3 = R2[:, 0:3 * SC * D // 2].bitcast(BF16).rearrange("p (s k d) -> p s k d", s=3, k=SC)
        Yw = XpT.rearrange("p c s -> p (c s)").rearrange("p (k d) -> p k d", k=SC)
        w3 = R2[:, 15360:15360 + B * 48].bitcast(BF16).rearrange("p (b e) -> p b e", b=B)
        slot_of = R2[:, 15744:15744 + SC * E1].rearrange("p (k e) -> p k e", k=SC)
        wslot = R2[:, 16064:16064 + SC]
        wr0 = wraw[0][:, :, :, :].rearrange("p a c d -> p (a c d)")
        rs1 = wr0[:, 0:256].rearrange("p (b e) -> p b e", b=B)
        sb1 = wr0[:, 256:512].rearrange("p (b e) -> p b e", b=B)
        mk1 = wr0[:, 512:512 + B * 36].rearrange("p (b e) -> p b e", b=B)
        rp1 = wr0[:, 800:800 + B * 36].rearrange("p (b e) -> p b e", b=B)
        gt1 = wr0[:, 1088:1344].rearrange("p (b e) -> p b e", b=B)
        vl1 = wr0[:, 1344:1600].rearrange("p (b e) -> p b e", b=B)
        gs1 = wr0[:, 1600:1600 + B * 13].rearrange("p (b e) -> p b e", b=B)
        gp1 = wr0[:, 1704:1704 + B * 13].rearrange("p (b e) -> p b e", b=B)
        m81 = wr0[:, 1808:1872].rearrange("p (b e) -> p b e", b=B)
        mg1 = wr0[:, 1872:1936].rearrange("p (b e) -> p b e", b=B)
        su1 = wr0[:, 1936:1944]
        rc1 = wr0[:, 1944:1952]
        Pb = sb("Pb", [P, 2, 8, P])
        PT = sb("PT", [P, 4, 4 * P])
        PTh = PT[:, :, :].rearrange("p a k -> p (a k)").bitcast(F16).rearrange("p (n s k) -> p n s k", n=2, s=2)

        xs = [CR_ for CR_ in (
            PT[:, 0:2, :].rearrange("p a k -> p (a k)").bitcast(BF16).rearrange("p (b d) -> p b d", b=B),
            PT[:, 2:4, :].rearrange("p a k -> p (a k)").bitcast(BF16).rearrange("p (b d) -> p b d", b=B),
            Pb[:, 0, :, :].rearrange("p h k -> p (h k)").bitcast(BF16).rearrange("p (b d) -> p b d", b=B))]
        xres = wraw[1][:, :, :, :].rearrange("p a c d -> p (a c d)").rearrange("p (b d) -> p b d", b=B)
        pb1 = Pb[:, 1, :, :].rearrange("p h k -> p (h k)")
        big1 = pb1[:, 0:128].rearrange("p (g a) -> p g a", a=2)
        small1 = pb1[:, 128:256].rearrange("p (g a) -> p g a", a=2)
        t1 = pb1[:, 256:320]
        t2 = pb1[:, 320:448].rearrange("p (g a) -> p g a", a=2)
        sel1 = pb1[:, 448:704].rearrange("p (b e) -> p b e", b=B)
        selb1 = pb1[:, 704:832].bitcast(BF16).rearrange("p (b e) -> p b e", b=B)
        gmask1 = pb1[:, 832:896].rearrange("p (b g) -> p b g", b=B)
        wtmp = vl1
        wprod = wr0[:, 0:480].rearrange("p (k s e) -> p k s e", k=5, s=3)
        gact = ctxT[:, 0, :].rearrange("p (n t) -> p n t", n=2)
        uact = ctxT[:, 1, :].rearrange("p (n t) -> p n t", n=2)
        hs = CT[:, :, :].rearrange("p b d -> p (b d)").rearrange("p (c t) -> p c t", c=DC)
        esig = xnT[:, 0, 0:640].rearrange("p (n s) -> p n s", n=4)
        eh = xnT[:, 1, 0:640].rearrange("p (n s) -> p n s", n=4)

        ctxR = Pb[:, :, :, :].rearrange("p a h k -> p a (h k)")
        CR = PT[:, :, :].rearrange("p a k -> p (a k)").rearrange("p (b d) -> p b d", b=B)

        def backwards(t, n):
            last = t[:, P - 1:P]
            return bass.AP(last.tensor, last.offset, [last.ap[0], [P, n], [-1, P]])

        PS = ctx.enter_context(nc.psum_tensor("PS", [P, 8, 512], F32))

        def bank(i, n=512, parts=P):
            return PS[0:parts, i, 0:n]

        kscr = nc.dram_tensor("kscr", (CH, P + D), F32, kind="Internal").ap()

        qk_scr = [nc.dram_tensor(f"qk_scr{i}", (4, D, T), F16, kind="Internal").ap() for i in range(3)]

        out_v = out.rearrange("b t d -> t b d")

        SELF0 = dict(n="a0", H=16, dv=16, upb=2, raw=0, sc=0.25, qb=0, vb=None, ob=0, KS=KSa)
        SELF1 = dict(n="a1", H=16, dv=16, upb=2, raw=1, sc=0.25, qb=1, vb=1, ob=2, KS=KSb)
        CROSS = dict(n="ax", H=32, dv=8, upb=4, raw=0, sc=float(8.0 ** -0.5), qb=2, vb=3, ob=4, KS=KSb)
        ATTENTIONS = [SELF0, SELF1, CROSS]

        def past(c, event):
            total = 0
            for a in ATTENTIONS[:ATTENTIONS.index(c)]:
                units = a["upb"] * B
                total += {"wt": 4, "wt_ps": 4, "qk_ps": jobs(a), "qk_hi": jobs(a), "qk": jobs(a), "ones": 1,
                          "stacked": 16 * 12 * (2 if a is CROSS else 1), "parked": 16 * 4 * NH,
                          "s": units, "sub": units, "exph": units, "exp": units, "pl": units, "pv": units,
                          "pt": units, "ptl": units, "pt_ps": 2 * units}.get(event, B)
            return total

        def jobs(c):
            return NH * (3 if c is CROSS else 4)

        def job_list(c):
            one = [(0, 0), (0, 1), (1, 0)] + ([] if c is CROSS else [(1, 1)])
            return [(half, w, cc) for half in range(NH) for w, cc in one]

        def unit_heads(c, u):
            if c is CROSS:
                rp, gh = divmod(u % 4, 2)
                return [(4 * (4 * gh + j) + 2 * rp + k, 32 * (2 * rp + k), 24, 4 * gh + j)
                        for k in range(2) for j in range(4)]
            return [(8 * (u % 2) + 2 * j + k, 64 * k, 48, 4 * (u % 2) + j) for k in range(2) for j in range(4)]

        def kv_head(c, h):
            return h // 4 if c["n"] == "ax" else h

        TURN = [0, 2, 4, 0, 0, 0]
        GE = 4
        NGR = E1 // GE
        GS = GE * CAP

        block = ctx.enter_context(nc.Block())

        @block.sync
        def _(sp):
            tot = {}

            def load(dst, src, sem, **kw):
                tot[sem] = tot.get(sem, 0) + 16
                sp.dma_start(dst, src, **kw).then_inc(S(sem), 16)

            def load_w(i, slot, w, sem):
                tot[sem] = tot.get(sem, 0) + 16
                sp.dma_start(wraw[i][:, slot, :, :], w.rearrange("(c p) i -> p c i", p=P)).then_inc(S(sem), 16)

            for b in range(B):
                load(X[:, b, :], A["x"][b], f"x_loaded{b}")
            for j, w in enumerate("qkvo"):
                load_w(0, j, A[f"L0_attn_W{w}"], "w_a0")
            load(bbc[:, 0, :], A["L0_attn_bo"].partition_broadcast(P), "bo_a0")
            load(kin[:, :], A["L0_xattn_k"], "k_loaded")
            load(CT[:, :, :], A["ctx_2048"].rearrange("b t d -> t b d"), "ctx_loaded")
            sp.wait_ge(S("krev_ready"), 1)
            load(kscr, krev[:, :], "kscr_written")
            sp.wait_ge(S("kscr_written"), 16)
            load(Toe[:, :, :], bass.AP(kscr.tensor, 0, [[1, P], [P + D, CH], [1, D]]), "toe_loaded")
            load(skip[:, :], A["fside_S2_0"].rearrange("(p a) -> p a", a=1), "skip_loaded")
            load_w(1, 0, A["L1_attn_Wq"], "w_a1")
            for j, w in list(enumerate("qkvo"))[1:]:
                load_w(1, j, A[f"L1_attn_W{w}"], "w_a1")
            for j, (n, k) in enumerate([("attn", "q"), ("attn", "k")]):
                for cc in range(DC):
                    load(bcol[:, 1, 2 * j + cc:2 * j + cc + 1],
                         A[f"L1_{n}_b{k}"][cc * P:(cc + 1) * P].rearrange("(p a) -> p a", a=1), "b_a1")
            load(bbc[:, 1, :], A["L1_attn_bv"].partition_broadcast(P), "b_a1")
            load(bbc[:, 2, :], A["L1_attn_bo"].partition_broadcast(P), "b_a1")

            def stack(c):
                scr = qk_scr[ATTENTIONS.index(c)]
                dv = c["dv"]
                tiles = 4 if c is CROSS else 2
                pitch = P // tiles
                for half in range(NH):
                    ts = slice(half * HF, (half + 1) * HF)
                    sp.wait_ge(S("att_qk"), past(c, "qk") + (half + 1) * jobs(c) // NH)
                    for part in range(4):
                        if c is CROSS and part >= 2:
                            sp.dma_start(scr[part, 0:64, ts], pair[0:64, part, 0, ts]).then_inc(S("att_parked"), 16)
                        else:
                            sp.dma_start(scr[part, :, ts].rearrange("(c p) t -> p c t", p=P),
                                         pair[:, part, :, ts]).then_inc(S("att_parked"), 16)
                    sp.wait_ge(S("att_parked"), past(c, "parked") + 64 * (half + 1))
                    for tile in range(tiles):
                        for w, parts in ((0, (0, 0, 1)), (1, (2, 3, 2))):
                            for term, part in enumerate(parts):
                                row = pitch * tile + dv * term
                                if w == 1 and c is CROSS:
                                    src = scr[part, 0:64, ts].rearrange("(g d) t -> d g t", g=8)
                                else:
                                    src = scr[part, :, ts].rearrange("(g s d) t -> s d g t", g=8, s=tiles)[tile]
                                dst = (QS, c["KS"])[w]
                                sp.dma_start(dst[row:row + dv, :, ts], src).then_inc(S(f"att_stacked{half}"), 16)

            stack(SELF0)
            sp.wait_ge(S("att_s"), 2 * B)
            for c in range(DC if stages >= 2 else 0):
                load(W1[:, c, 0:NS * FF].rearrange("p (n f) -> p n f", n=NS),
                     A["L0_ffn_shared_w1"][:, c * P:(c + 1) * P, :].rearrange("n p f -> p n f"), "w_e0")
                load(W1[:, c, NS * FF:F0].rearrange("p (n f) -> p n f", n=NR),
                     A["L0_ffn_routed_w1"][:, c * P:(c + 1) * P, :].rearrange("n p f -> p n f"), "w_e0")
            sw2 = A["L0_ffn_shared_w2"].rearrange("n f d -> (n f) d")
            rw2 = A["L0_ffn_routed_w2"].rearrange("n f d -> (n f) d")
            full = NS * FF // P
            rem = NS * FF - full * P
            mid = NB0 - 2 - full
            load(W2[:, 0:full, :], sw2[0:full * P].rearrange("(k p) d -> p k d", p=P), "w_e0")
            load(W2[0:rem, full, :], sw2[full * P:NS * FF], "w_e0")
            load(W2[rem:P, full, :], rw2[0:P - rem], "w_e0")
            load(W2[:, full + 1:full + 1 + mid, :],
                 rw2[P - rem:P - rem + mid * P].rearrange("(k p) d -> p k d", p=P), "w_e0")
            load(W2[0:LAST0, NB0 - 1, :], rw2[P - rem + mid * P:NR * FF], "w_e0")
            sp.wait_ge(S("b1row_cleared"), 1)
            sb1 = A["L0_ffn_shared_b1"].rearrange("n f -> (n f)")
            rb1 = A["L0_ffn_routed_b1"].rearrange("n f -> (n f)")

            def row(v):
                return v.rearrange("(a f) -> a f", a=1)
            load(b1row[0:full, :], sb1[0:full * P].rearrange("(k p) -> k p", p=P), "b_e0")
            load(b1row[full:full + 1, 0:rem], row(sb1[full * P:NS * FF]), "b_e0")
            load(b1row[full:full + 1, rem:P], row(rb1[0:P - rem]), "b_e0")
            load(b1row[full + 1:full + 1 + mid, :],
                 rb1[P - rem:P - rem + mid * P].rearrange("(k p) -> k p", p=P), "b_e0")
            load(b1row[NB0 - 1:NB0, 0:LAST0], row(rb1[P - rem + mid * P:NR * FF]), "b_e0")
            load(b2cat[0:NS, :], A["L0_ffn_shared_b2"], "b_e0")
            load(b2cat[NS:NE0, :], A["L0_ffn_routed_b2"], "b_e0")
            load(cen_raw[:, :], A["L0_ffn_centroids"], "b_e0")
            load(bias0[:, :], A["L0_ffn_bias"].partition_broadcast(P), "b_e0")
            for cc in range(DC):
                load(bcol[:, 2, cc:cc + 1], A["L1_xattn_bq"][cc * P:(cc + 1) * P].rearrange("(p a) -> p a", a=1), "b_ax")
            load(bcol[0:64, 2, 2:3], A["L1_xattn_bk"].rearrange("(p a) -> p a", a=1), "b_ax")
            load(bbc[:, 3, 0:64], A["L1_xattn_bv"].partition_broadcast(P), "b_ax")
            load(bbc[:, 4, :], A["L1_xattn_bo"].partition_broadcast(P), "b_ax")
            load(mq8[:, :], A["mask_SxS2_bc0"], "b_ax")
            load(mk8[:, :, :], A["mask_BxS2_bk0"].partition_broadcast(P), "b_ax")
            if stages >= 4:
                sp.wait_ge(S("x_updated"), 3 * B)
                load_w(0, 0, A["L1_xattn_Wq"], "w_ax")
                load(wraw[0][0:64, 1, 0, :], A["L1_xattn_Wk"], "w_ax")
                load(wraw[0][0:64, 2, 0, :], A["L1_xattn_Wv"], "w_ax")
                load_w(0, 3, A["L1_xattn_Wo"], "w_ax")
                load(rw_raw[:, :], A["L1_ffn_router_w"], "b_e1")
                load(ebias[:, :], A["L1_ffn_e_bias"].partition_broadcast(P), "b_e1")
            if stages >= 4:
                stack(SELF1)
                sp.wait_ge(S("att_wt"), 8)
                load_w(1, 0, A["L1_ffn_shared_gate"], "w_s1")
                load_w(1, 1, A["L1_ffn_shared_up"], "w_s1")
                load_w(1, 2, A["L1_ffn_shared_down"], "w_s1")
                for e in range(E1 if stages >= 6 else 0):
                    if e == WRING:
                        stack(CROSS)
                    if e >= WRING and e % GE == 0:
                        sp.wait_ge(S("y_ps"), (e - WRING) // GE + 1)
                    sl = e % WRING
                    for k, w in enumerate(("W_gate", "W_up")):
                        load(EW[:, sl, k * D:(k + 1) * D].rearrange("p (c i) -> p c i", c=DC),
                             A[f"L1_ffn_{w}"][e].rearrange("(c p) i -> p c i", p=P), f"ew{sl // GE}")
                    load(EW[:, sl, 2 * D:3 * D], A["L1_ffn_W_down"][e], f"ew{sl // GE}")
            if stages == 5:
                stack(CROSS)
            for b in range(B):
                sp.wait_ge(S("x_updated"), stages * B + b + 1 - B)
                sp.dma_start(out_v[:, b, :], X[:, b, :]).then_inc(S("stored"), 16)
            sp.wait_ge(S("stored"), 16 * B)
            if stages < 6:
                for k, n in tot.items():
                    sp.wait_ge(S(k), n)

        @block.gpsimd
        def _(pool):
            chain = [0]

            def link(ins):
                chain[0] += 1
                ins.then_inc(S("pool_chain"), 1)
                pool.wait_ge(S("pool_chain"), chain[0])

            g = nc.gpsimd
            link(g.memset(krev[:, D:D + P], 0.0))
            pool.wait_ge(S("k_loaded"), 16)
            g.tensor_copy(krev[:, 0:D], bass.AP(kin[:, D - 1:D].tensor, kin[:, D - 1:D].offset,
                                                [kin[:, D - 1:D].ap[0], [-1, D]])).then_inc(S("krev_ready"), 1)
            link(g.memset(mhalf[:, :], -0.5))

            def rstd_of(stage, b):
                pool.wait_ge(S("var_ready"), stage * B + b + 1)
                link(g.tensor_scalar(veps[:, b:b + 1], mv[:, b, 1:2], EPS, None, ALU.add))
                g.tensor_tensor(rstd[:, b:b + 1], veps[:, b:b + 1], mhalf[:, :],
                                ALU.pow).then_inc(S("rstd_ready"), 1)

            def rstds(stage, then=None):
                for b in range(B + 1):
                    if b < B:
                        rstd_of(stage, b)
                    if b >= 1 and then:
                        then(b - 1)

            def band(t, v, lo, hi, pattern, mult=1, fill0=1.0):
                link(g.memset(v, 1.0))
                link(g.affine_select(out=v, in_=v, compare_op=ALU.is_ge, fill=0.0, base=lo,
                                     pattern=pattern, channel_multiplier=mult))
                return g.affine_select(out=v, in_=v, compare_op=ALU.is_ge, fill=0.0, base=hi,
                                       pattern=[[-s, n] for s, n in pattern], channel_multiplier=-mult)

            link(g.memset(ident[:, :], 0.0))
            g.affine_select(out=ident[:, :], in_=ident[:, :], compare_op=ALU.not_equal, fill=1.0, base=0,
                            pattern=[[-1, P]], channel_multiplier=1).then_inc(S("const"), 1)
            link(g.memset(identb[:, :], 0.0))
            g.affine_select(out=identb[:, :], in_=identb[:, :], compare_op=ALU.not_equal, fill=1.0, base=0,
                            pattern=[[-1, P]], channel_multiplier=1).then_inc(S("const"), 1)
            pool.wait_ge(S("const"), 1)
            link(g.memset(causal[:, :], 0.0))
            g.affine_select(out=causal[:, :], in_=causal[:, :], compare_op=ALU.is_ge, fill=NEG, base=0,
                            pattern=[[-1, P]], channel_multiplier=1).then_inc(S("const"), 1)
            g.tensor_copy(identh[:, :], ident[:, :]).then_inc(S("const"), 1)
            g.memset(bcol[:, 0, :], 0.0).then_inc(S("const"), 1)
            band(chgroup, chgroup[:, :].rearrange("p (a i) -> p a i", a=CH), 0, CI - 1,
                 [[-CI, CH], [0, CI]]).then_inc(S("const"), 1)
            link(g.memset(onesb[:, :], 1.0))
            g.affine_select(out=before[:, :], in_=onesb[:, :], compare_op=ALU.is_ge, fill=0.0, base=-1,
                            pattern=[[1, P]], channel_multiplier=-1).then_inc(S("const"), 1)
            g.iota(slot_iota[:, :], pattern=[[1, CAP]], base=-1000, channel_multiplier=0,
                   allow_small_or_imprecise_dtypes=True).then_inc(S("const"), 1)

            def add_row(c, stage, b):
                sem, n = ("bo_a0", 16) if c["n"] == "a0" else ("b_a1", 96) if c["n"] == "a1" else ("b_ax", 16 * 7)
                pool.wait_ge(S(sem), n)
                pool.wait_ge(S("ln_done"), stage * B + b + 1)
                g.tensor_tensor(X[:, b, :], X[:, b, :], bbc[:, c["ob"], :], ALU.add).then_inc(S("x_biased"), 1)

            def low_parts(c, next_stage, then=None):
                cross = c is CROSS
                V, nkv, dv = (V8, 8, 8) if cross else (V16, 16, 16)
                for b in range(B):
                    pool.wait_ge(S("att_vh"), past(c, "vh") + b + 1)
                    g.tensor_tensor(V[1][:, b, :, 0:dv], vf[:, b % 2, 0:nkv * dv].rearrange("p (h e) -> p h e", h=nkv),
                                    V[0][:, b, :, 0:dv], ALU.subtract).then_inc(S("att_v"), 1)
                upb = c["upb"]
                U = upb * B
                for u in range(U + 9):
                    if u < U:
                        pool.wait_ge(S("att_exp"), past(c, "exp") + u + 1)
                        if u >= 4:
                            pool.wait_ge(S("att_pt_ps"), past(c, "pt_ps") + 2 * (u - 3))
                        g.tensor_tensor(Pl[:, u % 4, :, :], Pb[:, u % 2, :, :], Ph[:, u % 4, :, :],
                                        ALU.subtract).then_inc(S("att_pl"), 1)
                    if next_stage >= stages:
                        continue
                    if 0 <= u - 7 < U and (u - 7) % upb == upb - 1:
                        rstd_of(next_stage, (u - 7) // upb)
                    if 0 <= u - 9 < U and (u - 9) % upb == upb - 1 and then:
                        then((u - 9) // upb)

            rstds(0, lambda b: add_row(SELF0, 0, b))
            pool.wait_ge(S("att_wt"), 4)
            for part in range(3):
                band(sel, sel[part * GROUP:(part + 1) * GROUP, :], 0, FF - 1, [[1, F0]],
                     mult=-FF).then_inc(S("sel_ready"), 1)
                pool.wait_ge(S("sel_ready"), part + 1)
            low_parts(SELF0, 1)
            if stages < 2:
                return
            pool.wait_ge(S("ctx_loaded"), 16)
            pool.wait_ge(S("att_pv"), past(SELF1, "pv"))
            for b in range(B):
                g.tensor_copy(CR[:, b, :].rearrange("p (c l) -> p c l", c=DC), backwards(CT[:, b, :], DC)).then_inc(S("CR_ready"), 1)
            pool.wait_ge(S("xnT_ready"), 2 * B)
            pool.wait_ge(S("ctxT_ready"), B)
            for h in range(CH):
                if h >= 2:
                    pool.wait_ge(S("conv_done"), 2 * (h - 1))
                for m in range(DC):
                    v = xnT[:, m, :].rearrange("p (b c) -> p b c", b=B)[:, :, h * CI:(h + 1) * CI]
                    k = ctxT[:, m, :].rearrange("p (b c) -> p b c", b=B)[:, :, h * CI:(h + 1) * CI]
                    g.tensor_tensor(kv[:, h % 2, m, :].rearrange("p (b i j) -> p b i j", b=B, i=CI),
                                    v.unsqueeze(3).broadcast_to([P, B, CI, CI]),
                                    k.unsqueeze(2).broadcast_to([P, B, CI, CI]),
                                    ALU.mult).then_inc(S("kv_ready"), 1)
            for b in range(B):
                pool.wait_ge(S("wb_ready"), b + 1)
                g.tensor_tensor(X[:, b, :], X[:, b, :], wb[:, b, :], ALU.add).then_inc(S("x_skip"), 1)
            if stages < 3:
                return
            def flat(b):
                pool.wait_ge(S("ln_done"), 2 * B + b + 1)
                g.tensor_tensor(X[:, b, :], X[:, b, :], xn[:, b, :], ALU.add).then_inc(S("x_flat"), 1)
            rstds(2, flat)
            if stages < 4:
                return
            rstds(3, lambda b: add_row(SELF1, 3, b))
            low_parts(SELF1, 4, lambda b: add_row(CROSS, 4, b))
            if stages < 5:
                return
            low_parts(CROSS, 5)
            if stages < 6:
                return
            pool.wait_ge(S("att_proj"), 3 * B)
            band(slot_of, slot_of, 0, CAP - 1, [[P, SC], [-CAP, E1]]).then_inc(S("slot_of"), 1)
            pool.wait_ge(S("wt_s1"), 4)
            for b in range(B):
                pool.wait_ge(S("xs_hi"), b + 1)
                g.tensor_tensor(xres[:, b, :], xn[:, b, :], xs[0][:, b, :], ALU.subtract).then_inc(S("xs_res"), 1)
            for b in range(B):
                pool.wait_ge(S("xs_mid"), b + 1)
                g.tensor_tensor(xs[2][:, b, :], xres[:, b, :], xs[1][:, b, :], ALU.subtract).then_inc(S("xs_lo"), 1)
            for j in range(NH * DC):
                half, ic = divmod(j, DC)
                pool.wait_ge(S("s_up"), j + 1)
                g.tensor_tensor(hs[:, ic, half * HF:(half + 1) * HF], gact[:, j % 2, :], uact[:, j % 2, :],
                                ALU.mult).then_inc(S("hs"), 1)
            for k in range(SC):
                pool.wait_ge(S("y_hi"), k + 1)
                g.tensor_tensor(Yw[:, k, :], Yw[:, k, :], Y3[:, 0, k, :], ALU.subtract).then_inc(S("y_res"), 1)
                if k >= 1:
                    pool.wait_ge(S("y_mid"), k)
                    g.tensor_tensor(Y3[:, 2, k - 1, :], Yw[:, k - 1, :], Y3[:, 1, k - 1, :], ALU.subtract).then_inc(S("y_lo"), 1)
            pool.wait_ge(S("y_mid"), SC)
            g.tensor_tensor(Y3[:, 2, SC - 1, :], Yw[:, SC - 1, :], Y3[:, 1, SC - 1, :], ALU.subtract).then_inc(S("y_lo"), 1)

        @block.scalar
        def _(act):
            s = nc.scalar
            chain = [0]

            def link(ins):
                chain[0] += 1
                ins.then_inc(S("act_chain"), 1)
                act.wait_ge(S("act_chain"), chain[0])

            def xnt(stage):
                for b in range(B):
                    act.wait_ge(S("xnT_ps"), stage * B + b + 1)
                    s.activation(xnT[:, :, b * P:(b + 1) * P],
                                 bank(TURN[stage] + b % 2, 256).rearrange("p (c t) -> p c t", c=DC),
                                 ACT.Copy).then_inc(S("xnT_ready"), 1)

            def weights(c):
                n = c["n"]
                for w in range(4):
                    act.wait_ge(S("att_wt_ps"), past(c, "wt_ps") + w + 1)
                    src = bank(w).rearrange("p (c o) -> p c o", c=DC)
                    if n != "ax" or w in (0, 3):
                        s.activation(WT[:, w, :, :], src, ACT.Copy).then_inc(S("att_wt"), 1)
                    else:
                        s.activation(WT[:, w, :, 0:64], src[:, :, 0:64], ACT.Copy).then_inc(S("att_wt"), 1)

            def attention(c, stage):
                n, H, dv, upb = c["n"], c["H"], c["dv"], c["upb"]
                cross = n == "ax"
                weights(c)
                xnt(stage)
                if c is SELF0:
                    act.wait_ge(S("const"), 5)
                else:
                    act.wait_ge(S(f"b_{n}"), 96 if n == "a1" else 16 * 7)
                for i, (half, w, cc) in enumerate(job_list(c)):
                    m = 64 if cross and w else P
                    act.wait_ge(S("att_qk_ps"), past(c, "qk_ps") + i + 1)
                    s.activation(pair[0:m, 2 * w, cc, half * HF:(half + 1) * HF], bank(i % 4, parts=m), ACT.Identity,
                                 bias=bcol[0:m, c["qb"], 2 * w + cc:2 * w + cc + 1]).then_inc(S("att_qk_hi"), 1)
                V, nkv = (V8, 8) if cross else (V16, 16)
                for b in range(B):
                    act.wait_ge(S("att_vf"), past(c, "vf") + b + 1)
                    s.activation(V[0][:, b, :, 0:dv], vf[:, b % 2, 0:nkv * dv].rearrange("p (h e) -> p h e", h=nkv),
                                 ACT.Copy).then_inc(S("att_vh"), 1)
                U = upb * B
                for half in range(NH):
                    act.wait_ge(S(f"att_stacked{half}"), past(c, "stacked") + (384 if cross else 192))
                for u in range(U + 8):
                    if u < U:
                        act.wait_ge(S("att_sub"), past(c, "sub") + u + 1)
                        if u >= 4:
                            act.wait_ge(S("att_pt_ps"), past(c, "pt_ps") + 2 * (u - 3) - 1)
                        s.activation(Ph[:, u % 4, :, :], Pb[:, u % 2, :, :], ACT.Exp, scale=c["sc"]).then_inc(S("att_exph"), 1)
                        act.wait_ge(S("att_exph"), past(c, "exph") + u + 1)
                        s.activation(Pb[:, u % 2, :, :], Pb[:, u % 2, :, :], ACT.Exp, scale=c["sc"]).then_inc(S("att_exp"), 1)
                    t = u - 3
                    if 0 <= t < U:
                        if t >= 2:
                            act.wait_ge(S("att_pv"), past(c, "pv") + t - 1)
                        act.wait_ge(S("att_pt_ps"), past(c, "pt_ps") + 2 * t + 2)
                        s.activation(PTh[:, t % 2, 1, :], PS[:, 5, :].bitcast(F16), ACT.Copy).then_inc(S("att_ptl"), 1)
                    f = u - 6
                    if f >= 0 and f < U and f % upb == upb - 1:
                        act.wait_ge(S("att_attT_ps"), past(c, "attT_ps") + f // upb + 1)
                        s.activation(attT[:, :, :], bank(7, 256).rearrange("p (c t) -> p c t", c=DC),
                                     ACT.Copy).then_inc(S("att_attT"), 1)

            attention(SELF0, 0)
            if stages < 2:
                return
            for b in range(B):
                act.wait_ge(S("ctxT_ps"), b + 1)
                s.activation(ctxT[:, :, b * P:(b + 1) * P], bank(4 + b % 2, 256).rearrange("p (c t) -> p c t", c=DC),
                             ACT.Copy).then_inc(S("ctxT_ready"), 1)
            for b in range(B):
                act.wait_ge(S("ctxR_ps"), b + 1)
                s.activation(ctxR[:, :, b * P:(b + 1) * P], bank(4 + b % 2, 256).rearrange("p (c t) -> p c t", c=DC),
                             ACT.Copy).then_inc(S("ctxR_ready"), 1)
            xnt(1)
            if stages < 3:
                return
            act.wait_ge(S("small_e0_ps"), 1)
            s.activation(cenT[:, :, :], bank(0, 32).rearrange("p (c e) -> p c e", c=DC), ACT.Copy).then_inc(S("small_e0"), 1)
            s.activation(b1col[:, :], PS[:, 0, 64:64 + NB0], ACT.Copy).then_inc(S("small_e0"), 1)
            xnt(2)
            act.wait_ge(S("score0_ps"), 1)
            s.activation(rs0, bank(2, B * NR).rearrange("p (b e) -> p b e", b=B), ACT.Sigmoid).then_inc(S("score0"), 1)
            for b in range(B):
                act.wait_ge(S("g3T_ps"), b + 1)
                link(s.activation(g3T[0:96, b * P:(b + 1) * P], PS[0:96, b % 2, 0:P], ACT.Copy))
                s.activation(g0T[:, b * P:(b + 1) * P], PS[0:NE0, b % 2, P:2 * P], ACT.Copy).then_inc(S("g3T"), 1)
            for i in range(NH * NB0):
                blk = i % NB0
                m = P if blk < NB0 - 1 else LAST0
                act.wait_ge(S("up0_ps"), i + 1)
                if i >= 2:
                    act.wait_ge(S("hg"), i - 1)
                s.activation(hid[0:m, i % 2, :], bank(i % 2, parts=m), ACT.Relu,
                             bias=b1col[0:m, blk:blk + 1]).then_inc(S("hid"), 1)
            if stages < 4:
                return
            attention(SELF1, 3)
            if stages < 5:
                return
            attention(CROSS, 4)
            if stages < 6:
                return
            for w in range(3):
                act.wait_ge(S("wt_ps_s1"), w + 1)
                s.activation(WT[:, w, :, :], bank(w).rearrange("p (c o) -> p c o", c=DC), ACT.Copy).then_inc(S("wt_s1"), 1)
            act.wait_ge(S("wt_ps_s1"), 4)
            s.activation(rwT[:, :, :], bank(3, 2 * E1).rearrange("p (c e) -> p c e", c=DC), ACT.Copy).then_inc(S("wt_s1"), 1)
            xnt(5)
            act.wait_ge(S("score1_ps"), 1)
            s.activation(rs1, bank(2, B * E1).rearrange("p (b e) -> p b e", b=B), ACT.Sigmoid).then_inc(S("score1"), 1)
            for b in range(B):
                s.activation(xs[0][:, b, :], xn[:, b, :], ACT.Copy).then_inc(S("xs_hi"), 1)

            def shared(j):
                act.wait_ge(S("s_ps"), j + 1)
                if j >= 2:
                    act.wait_ge(S("hs"), j - 1)
                s.activation(gact[:, j % 2, :], bank(4 + 2 * (j % 2)), ACT.Silu).then_inc(S("s_gate"), 1)
                s.activation(uact[:, j % 2, :], bank(5 + 2 * (j % 2)), ACT.Copy).then_inc(S("s_up"), 1)

            def mids(lo, hi):
                for b in range(lo, hi):
                    act.wait_ge(S("xs_res"), b + 1)
                    s.activation(xs[1][:, b, :], xres[:, b, :], ACT.Copy).then_inc(S("xs_mid"), 1)
            shared(0)
            shared(1)
            mids(0, B)
            shared(2)
            shared(3)
            act.wait_ge(S("gather_ps"), 1)
            for k, (e0, e1) in enumerate(ESPAN):
                n = (e1 - e0) * CAP
                s.activation(XpT[:, 0, e0 * CAP:e1 * CAP], bank(2 * k, n), ACT.Copy).then_inc(S("XpT_a"), 1)
            for gr in range(NGR):
                act.wait_ge(S("eup_ps"), gr + 1)
                s.activation(esig[:, gr % 4, :], bank(gr % 2, GS), ACT.Silu).then_inc(S("esig"), 1)
                for k in ([gr] if gr < NGR - 1 else range(gr, SC)):
                    act.wait_ge(S("PmT_ps"), k + 1)
                    s.activation(PmT[:, k, :], PS[:, 6 + k % 2, :].bitcast(BF16), ACT.Copy).then_inc(S("PmT"), 1)
            for k in range(SC):
                act.wait_ge(S("Y_ps"), k // 2 + 1)
                s.activation(Yw[:, k, :], PS[:, 4 + k // 2 % 2, (k % 2) * D:(k % 2 + 1) * D], ACT.Copy,
                             scale=wslot[:, k:k + 1]).then_inc(S("Yw"), 1)
                act.wait_ge(S("Yw"), k + 1)
                s.activation(Y3[:, 0, k, :], Yw[:, k, :], ACT.Copy).then_inc(S("y_hi"), 1)
                if k >= 1:
                    act.wait_ge(S("y_res"), k)
                    s.activation(Y3[:, 1, k - 1, :], Yw[:, k - 1, :], ACT.Copy).then_inc(S("y_mid"), 1)
            act.wait_ge(S("y_res"), SC)
            s.activation(Y3[:, 1, SC - 1, :], Yw[:, SC - 1, :], ACT.Copy).then_inc(S("y_mid"), 1)

        @block.vector
        def _(dve):
            v = nc.vector
            chain = [0]

            def link(ins):
                chain[0] += 1
                ins.then_inc(S("dve_chain"), 1)
                dve.wait_ge(S("dve_chain"), chain[0])

            pending = []

            def variance(b):
                link(v.bn_stats(stats[:, b, :], X[:, b, :]))
                v.bn_aggr(mv[:, b, :], stats[:, b, :]).then_inc(S("var_ready"), 1)
                pending.append(b)

            def normalize():
                while pending:
                    b = pending.pop(0)
                    rstds_seen[0] += 1
                    dve.wait_ge(S("rstd_ready"), rstds_seen[0])
                    v.tensor_scalar(xn[:, b, :], X[:, b, :], mv[:, b, 0:1], rstd[:, b:b + 1], ALU.subtract,
                                    ALU.mult).then_inc(S("ln_done"), 1)

            rstds_seen = [0]

            def update(b, stage, src):
                x = X[:, b, :]
                if len(src.shape) == 3:
                    x = x.rearrange("p (c l) -> p c l", c=DC)
                v.tensor_tensor(x, x, src, ALU.add).then_inc(S("x_updated"), 1)
                if stage + 1 < stages:
                    dve.wait_ge(S("x_updated"), stage * B + b + 1)
                    variance(b)

            v.memset(b1row[:, :], 0.0).then_inc(S("b1row_cleared"), 1)
            for b in range(B):
                dve.wait_ge(S(f"x_loaded{b}"), 16)
                variance(b)
                if b >= 1:
                    first = pending.pop()
                    normalize()
                    pending.append(first)
            normalize()
            def attention(c, stage):
                n, H, dv, upb = c["n"], c["H"], c["dv"], c["upb"]
                cross = n == "ax"
                V, nkv = (V8, 8) if cross else (V16, 16)
                v.memset(V[0][:, :, :, dv:dv + 1], 1.0)
                v.memset(V[1][:, :, :, dv:dv + 1], 0.0).then_inc(S("att_ones"), 1)
                if n == "a1":
                    dve.wait_ge(S("b_a1"), 96)
                if cross:
                    dve.wait_ge(S("b_ax"), 16 * 7)
                    link(v.tensor_tensor(xmask[:, :, :], mk8[:, :, :],
                                         mq8[:, :].unsqueeze(1).broadcast_to([P, B, P]), ALU.max))
                    v.tensor_scalar(xmask[:, :, :], xmask[:, :, :], NEG, None, ALU.mult).then_inc(S("xmask"), 1)
                for i, (half, w, cc) in enumerate(job_list(c)):
                    m = 64 if cross and w else P
                    ts = slice(half * HF, (half + 1) * HF)
                    dve.wait_ge(S("att_qk_hi"), past(c, "qk_hi") + i + 1)
                    v.scalar_tensor_tensor(pair[0:m, 2 * w + 1, cc, ts], bank(i % 4, parts=m),
                                           bcol[0:m, c["qb"], 2 * w + cc:2 * w + cc + 1],
                                           pair[0:m, 2 * w, cc, ts], ALU.add, ALU.subtract).then_inc(S("att_qk"), 1)
                for b in range(B):
                    dve.wait_ge(S("att_v_ps"), past(c, "v_ps") + b + 1)
                    if b >= 2:
                        dve.wait_ge(S("att_v"), past(c, "v") + b - 1)
                    if c["vb"] is None:
                        v.tensor_copy(vf[:, b % 2, :], bank(4 + b % 2, nkv * dv)).then_inc(S("att_vf"), 1)
                    else:
                        v.tensor_tensor(vf[:, b % 2, 0:nkv * dv], bank(4 + b % 2, nkv * dv), bbc[:, c["vb"], 0:nkv * dv],
                                        ALU.add).then_inc(S("att_vf"), 1)
                U = upb * B
                for u in range(U + 8):
                    f = u - 5
                    if 0 <= f < U and f % upb == upb - 1:
                        b = f // upb
                        o = bank(6, H * (dv + 1)).rearrange("p (h e) -> p h e", h=H)
                        dve.wait_ge(S("att_pv"), past(c, "pv") + f + 1)
                        link(v.reciprocal(rec[:, b % 2, 0:H], o[:, :, dv]))
                        v.tensor_tensor(att[:, b % 2, :].rearrange("p (h e) -> p h e", h=H), o[:, :, 0:dv],
                                        rec[:, b % 2, 0:H].unsqueeze(2).broadcast_to([P, H, dv]),
                                        ALU.mult).then_inc(S("att_att"), 1)
                    if u < U:
                        sc = PS[:, 2 * (u % 2):2 * (u % 2) + 2, :].rearrange("p a (h k) -> p (a h) k", h=4)
                        dve.wait_ge(S("att_s"), past(c, "s") + u + 1)
                        link(v.tensor_reduce(mx[:, u % 2, :], sc, AX.X, ALU.max))
                        if u >= 2:
                            dve.wait_ge(S("att_pl"), past(c, "pl") + u - 1)
                        v.tensor_tensor(Pb[:, u % 2, :, :], sc, mx[:, u % 2, :].unsqueeze(2).broadcast_to([P, 8, P]),
                                        ALU.subtract).then_inc(S("att_sub"), 1)
                    t = u - 3
                    if 0 <= t < U:
                        if t >= 2:
                            dve.wait_ge(S("att_pv"), past(c, "pv") + t - 1)
                        dve.wait_ge(S("att_pt_ps"), past(c, "pt_ps") + 2 * t + 1)
                        v.tensor_copy(PTh[:, t % 2, 0, :], PS[:, 4, :].bitcast(F16)).then_inc(S("att_pt"), 1)
                    normalize()
                    f = u - 7
                    if 0 <= f < U and f % upb == upb - 1:
                        b = f // upb
                        dve.wait_ge(S("att_proj"), past(c, "proj") + b + 1)
                        dve.wait_ge(S("x_biased"), [0, 0, 0, 1, 2][stage] * B + b + 1)
                        update(b, stage, PS[:, 7, 256:512])
                normalize()

            attention(SELF0, 0)
            if stages < 2:
                return
            dve.wait_ge(S("ctx_loaded"), 16)
            dve.wait_ge(S("skip_loaded"), 16)
            dve.wait_ge(S("ln_done"), 2 * B)
            for b in range(B):
                v.scalar_tensor_tensor(ub[:, b, :], xn[:, b, :], skip[:, 0:1], CT[:, b, :], ALU.mult,
                                       ALU.mult).then_inc(S("ub"), 1)
            for b in range(B):
                dve.wait_ge(S("skip_ps"), b + 1)
                v.tensor_tensor(wb[:, b, :], CT[:, b, :], bank(4 + b % 2, 256), ALU.mult).then_inc(S("wb_ready"), 1)
            for h in range(CH):
                for m in range(DC):
                    i = DC * h + m
                    dve.wait_ge(S("conv_done"), i + 1)
                    x1 = ctxR[:, m, :].rearrange("p (b c) -> p b c", b=B)[:, :, h * CI:(h + 1) * CI]
                    z = zb[:, i % 4, :].rearrange("p (b i j) -> p b i j", b=B, i=CI)
                    v.tensor_tensor(z, bank(i % 4).rearrange("p (b i j) -> p b i j", b=B, i=CI),
                                    x1.unsqueeze(3).broadcast_to([P, B, CI, CI]), ALU.mult).then_inc(S("z"), 1)
                    dve.wait_ge(S("z"), i + 1)
                    v.tensor_reduce(oT[:, m, :].rearrange("p (b c) -> p b c", b=B)[:, :, h * CI:(h + 1) * CI],
                                    z.rearrange("p b i j -> p b j i"), AX.X, ALU.add).then_inc(S("oT"), 1)
            for b in range(B):
                dve.wait_ge(S("convT_ps"), b + 1)
                dve.wait_ge(S("x_skip"), b + 1)
                normalize()
                update(b, 1, backwards(bank(6 + b % 2, 256), DC))
            normalize()
            if stages < 3:
                return

            dve.wait_ge(S("b_e0"), 16 * 9)
            v.memset(sc0[:, :, NR:20], NEG).then_inc(S("pad0"), 1)
            link(v.memset(G3[:, :, :], 0.0))
            dve.wait_ge(S("score0"), 1)
            link(v.tensor_tensor(sc0[:, :, 0:NR], rs0, bias0[:, :].unsqueeze(1).broadcast_to([P, B, NR]), ALU.add))
            for b in range(B):
                ins = v.max(m80[:, b, :], sc0[:, b, 0:NR])
            link(ins)
            link(v.memset(m80[:, :, KR:8], NEG))
            dve.wait_ge(S("pad0"), 1)
            for b in range(B):
                ins = v.match_replace(out=rp0[:, b, :], in_to_replace=m80[:, b, :], in_values=sc0[:, b, :], imm_value=FAR)
            link(ins)
            link(v.tensor_tensor(gv0, rp0[:, :, 0:NR], sc0[:, :, 0:NR], ALU.not_equal))
            link(v.tensor_tensor(gv0, gv0, sc0[:, :, 0:NR], ALU.mult))
            link(v.tensor_reduce(gs0, gv0, AX.X, ALU.add))
            link(v.tensor_scalar(gs0, gs0, 1e-8, None, ALU.max))
            link(v.reciprocal(gr0, gs0))
            link(v.memset(gf0[:, :, 0:NS], 1.0))
            link(v.tensor_tensor(gf0[:, :, NS:NE0], gv0, gr0.unsqueeze(2).broadcast_to([P, B, NR]), ALU.mult))
            link(v.memset(G3[:, :, 0:NS], 1.0))
            for part in range(3):
                lo = part * GROUP + NS
                link(v.tensor_copy(gb0, gf0[:, :, NS:NE0] if part == 0 else gv0))
                link(v.tensor_copy(G3[:, :, lo:lo + NR], gb0))
                if part < 2:
                    link(v.tensor_tensor(gv0, gf0[:, :, NS:NE0] if part == 0 else gv0, gb0, ALU.subtract))
            v.tensor_copy(m80[:, 0, 0:1], m80[:, 0, 1:2]).then_inc(S("G3"), 1)
            for i in range(NH * NB0):
                m = P if i % NB0 < NB0 - 1 else LAST0
                dve.wait_ge(S("hid"), i + 1)
                dve.wait_ge(S("gate_ps"), i + 1)
                if i >= 2:
                    dve.wait_ge(S("down0"), i - 1)
                v.tensor_tensor(hg[0:m, i % 2, :], hid[0:m, i % 2, :], bank(2 + i % 2, parts=m),
                                ALU.mult).then_inc(S("hg"), 1)
                if i % NB0 == NB0 - 1:
                    half = i // NB0
                    dve.wait_ge(S("down0"), i + 1)
                    for t in range(4):
                        b = 4 * half + t
                        dve.wait_ge(S("x_flat"), b + 1)
                        normalize()
                        update(b, 2, bank(4 + t, 256))
            normalize()
            if stages < 4:
                return
            attention(SELF1, 3)
            if stages < 5:
                return
            attention(CROSS, 4)
            if stages < 6:
                return

            dve.wait_ge(S("b_e1"), 32)
            v.memset(gs1[:, :, NG1:13], NEG)
            link(v.memset(mk1[:, :, E1:36], NEG))
            dve.wait_ge(S("score1"), 1)
            link(v.tensor_tensor(sb1, rs1, ebias[:, :].unsqueeze(1).broadcast_to([P, B, E1]), ALU.add))
            pairs = sb1.rearrange("p b e -> p (b e)").rearrange("p (g a c) -> p g a c", a=2, c=2)
            v.tensor_reduce(big1, pairs, AX.X, ALU.max)
            link(v.tensor_reduce(small1, pairs, AX.X, ALU.min))
            v.tensor_tensor(t1, big1[:, :, 0], big1[:, :, 1], ALU.add)
            link(v.tensor_tensor(t2, big1, small1, ALU.add))
            link(v.tensor_tensor(t2[:, :, 0], t2[:, :, 0], t2[:, :, 1], ALU.max))
            link(v.tensor_tensor(gs1[:, :, 0:NG1], t2[:, :, 0].rearrange("p (b g) -> p b g", b=B),
                                 t1.rearrange("p (b g) -> p b g", b=B), ALU.max))
            for b in range(B):
                ins = v.max(mg1[:, b, :], gs1[:, b, 0:NG1])
            link(ins)
            link(v.memset(mg1[:, :, TKG:8], NEG))
            for b in range(B):
                ins = v.match_replace(out=gp1[:, b, :], in_to_replace=mg1[:, b, :], in_values=gs1[:, b, :], imm_value=FAR)
            link(ins)
            link(v.tensor_tensor(gmask1, gp1[:, :, 0:NG1], gs1[:, :, 0:NG1], ALU.not_equal))
            link(v.tensor_tensor(mk1[:, :, 0:E1].rearrange("p b (g k) -> p b g k", g=NG1),
                                 sb1.rearrange("p b (g k) -> p b g k", g=NG1),
                                 gmask1.unsqueeze(3).broadcast_to([P, B, NG1, E1 // NG1]), ALU.mult))
            for b in range(B):
                ins = v.max(m81[:, b, :], mk1[:, b, 0:E1])
            link(ins)
            link(v.memset(m81[:, :, K1:8], NEG))
            for b in range(B):
                ins = v.match_replace(out=rp1[:, b, :], in_to_replace=m81[:, b, :], in_values=mk1[:, b, :], imm_value=FAR)
            link(ins)
            link(v.tensor_tensor(sel1, rp1[:, :, 0:E1], mk1[:, :, 0:E1], ALU.not_equal))
            v.tensor_copy(selb1, sel1).then_inc(S("selb1"), 1)
            link(v.tensor_tensor(gt1, sel1, rs1, ALU.mult))
            link(v.tensor_reduce(su1, gt1, AX.X, ALU.add))
            link(v.tensor_scalar(su1, su1, 1e-20, None, ALU.add))
            link(v.reciprocal(rc1, su1))
            link(v.tensor_tensor(gt1, gt1, rc1.unsqueeze(2).broadcast_to([P, B, E1]), ALU.mult))
            link(v.tensor_scalar(gt1, gt1, SCALE1, None, ALU.mult))
            dve.wait_ge(S("rank_ps"), 1)
            link(v.scalar_tensor_tensor(vl1.rearrange("p b e -> p (b e)"), sel1.rearrange("p b e -> p (b e)"), -1000.0,
                                        bank(3, B * E1), ALU.mult, ALU.add))
            dve.wait_ge(S("att_proj"), 3 * B)
            for b in range(B):
                v.tensor_tensor(Pm[:, b, :].rearrange("p (e c) -> p e c", e=E1),
                                vl1[:, b, :].unsqueeze(2).broadcast_to([P, E1, CAP]),
                                slot_iota[:, :].unsqueeze(1).broadcast_to([P, E1, CAP]),
                                ALU.is_equal).then_inc(S("Pm"), 1)
            dve.wait_ge(S("Pm"), B)
            for part in range(3):
                link(v.tensor_copy(w3[:, :, part * E1:(part + 1) * E1], gt1))
                if part < 2:
                    link(v.tensor_tensor(gt1, gt1, w3[:, :, part * E1:(part + 1) * E1], ALU.subtract))
            v.memset(su1, 0.0).then_inc(S("w3"), 1)
            dve.wait_ge(S("gather_ps"), 1)
            for k, (e0, e1) in enumerate(ESPAN):
                v.tensor_copy(XpT[:, 1, e0 * CAP:e1 * CAP], bank(2 * k + 1, (e1 - e0) * CAP)).then_inc(S("XpT_v"), 1)
            dve.wait_ge(S("slot_of"), 1)
            for hb in range(2):
                dve.wait_ge(S("wslot_ps"), hb + 1)
                for k in range(5):
                    ins = v.tensor_tensor(wprod[:, k, :, :],
                                          PS[:, 6 + hb, k * 96:(k + 1) * 96].rearrange("p (s e) -> p s e", s=3),
                                          slot_of[:, 5 * hb + k, :].unsqueeze(1).broadcast_to([P, 3, E1]), ALU.mult)
                link(ins)
                v.tensor_reduce(wslot[:, 5 * hb:5 * hb + 5], wprod, AX.XY, ALU.add).then_inc(S("wslot"), 1)
                dve.wait_ge(S("wslot"), hb + 1)
            for gr in range(NGR):
                dve.wait_ge(S("esig"), gr + 1)
                v.tensor_tensor(eh[:, gr % 4, :], esig[:, gr % 4, :], PS[:, gr % 2, 256:256 + GS],
                                ALU.mult).then_inc(S("eh"), 1)
                if gr >= 1:
                    k = gr - 1
                    dve.wait_ge(S("y_ps"), k + 1)
                    v.tensor_copy(yT[:, :, k * GS:(k + 1) * GS], PS[:, 2 + k % 2, 0:2 * GS].rearrange("p (c s) -> p c s", c=DC)).then_inc(S("yT"), 1)
            k = NGR - 1
            dve.wait_ge(S("y_ps"), k + 1)
            v.tensor_copy(yT[:, :, k * GS:(k + 1) * GS], PS[:, 2 + k % 2, 0:2 * GS].rearrange("p (c s) -> p c s", c=DC)).then_inc(S("yT"), 1)
            for b in range(B):
                dve.wait_ge(S("e1_out"), b + 1)
                update(b, 5, bank(b % 4, 256))

        @block.tensor
        def _(pe):
            def mm(o_, l, r, start, stop):
                return nc.tensor.matmul(o_, l, r, start=start, stop=stop)

            def tr(o_, i_):
                k = i_.shape[0]
                return nc.tensor.transpose(o_, i_, ident[0:k, 0:k])

            def xnt(stage):
                for b in range(B):
                    pe.wait_ge(S("ln_done"), stage * B + b + 1)
                    i = stage * B + b
                    if b >= 2:
                        pe.wait_ge(S("xnT_ready"), i - 1)
                    for cc in range(DC):
                        ins = tr(PS[:, TURN[stage] + b % 2, cc * P:(cc + 1) * P], xn[:, b, cc * P:(cc + 1) * P])
                    ins.then_inc(S("xnT_ps"), 1)

            def weights(c):
                n, raw = c["n"], wraw[c["raw"]]
                pe.wait_ge(S(f"w_{n}"), 64)
                for w in range(4):
                    rows = 64 if n == "ax" and w in (1, 2) else D
                    for ic in range(DC):
                        for oc in range(-(-rows // P)):
                            k = min(P, rows - oc * P)
                            ins = tr(PS[:, w, ic * D + oc * P:ic * D + oc * P + k],
                                     raw[0:k, w, oc, ic * P:(ic + 1) * P])
                    ins.then_inc(S("att_wt_ps"), 1)

            def attention(c, stage):
                n, H, dv, upb = c["n"], c["H"], c["dv"], c["upb"]
                cross = n == "ax"
                V = V8 if cross else V16
                weights(c)
                pe.wait_ge(S("att_wt"), past(c, "wt") + 4)
                xnt(stage)
                src = ctxT if cross else xnT
                pe.wait_ge(S("xnT_ready"), stage * B + B)
                for i, (half, w, cc) in enumerate(job_list(c)):
                    m = 64 if cross and w else P
                    if i >= 4:
                        pe.wait_ge(S("att_qk"), past(c, "qk") + i - 3)
                    for dc in range(DC):
                        ins = mm(bank(i % 4, parts=m), WT[:, w, dc, cc * P:cc * P + m],
                                 (src if w else xnT)[:, dc, half * HF:(half + 1) * HF], dc == 0, dc == 1)
                    ins.then_inc(S("att_qk_ps"), 1)
                for b in range(B):
                    if b >= 2:
                        pe.wait_ge(S("att_vf"), past(c, "vf") + b - 1)
                    w = 64 if cross else D
                    for dc in range(DC):
                        ins = mm(bank(4 + b % 2, w), src[:, dc, b * P:(b + 1) * P], WT[:, 2, dc, 0:w], dc == 0, dc == 1)
                    ins.then_inc(S("att_v_ps"), 1)

                per_half = 384 if cross else 192

                def scores(u):
                    b = u // upb
                    if u % (upb * B // NH) == 0:
                        pe.wait_ge(S(f"att_stacked{u // (upb * B // NH)}"), past(c, "stacked") + per_half)
                    if u >= 2:
                        pe.wait_ge(S("att_sub"), past(c, "sub") + u - 1)
                    p0 = 2 * (u % 2)
                    mask = xmask[:, b, :] if cross else causal[:, :]
                    for k in range(2):
                        mm(bank(p0 + k), identb[:, :], mask.unsqueeze(1).broadcast_to([P, 4, P]), True, False)
                    ts = slice(b * P, (b + 1) * P)
                    for j in range(4):
                        for k in range(2):
                            _, row, rows, idx = unit_heads(c, u)[4 * k + j]
                            ins = mm(PS[:, p0 + k, j * P:(j + 1) * P], QS[row:row + rows, idx, ts],
                                     c["KS"][row:row + rows, idx, ts], False, j == 3)
                    ins.then_inc(S("att_s"), 1)

                def transposes(u):
                    for k, src_ in ((0, Ph), (1, Pl)):
                        pe.wait_ge(S(("att_exph", "att_pl")[k]), past(c, ("exph", "pl")[k]) + u + 1)
                        if u >= 1:
                            pe.wait_ge(S(("att_pt", "att_ptl")[k]), past(c, ("pt", "ptl")[k]) + u)
                        dst = PS[:, 4 + k, :].bitcast(F16)
                        for j in range(8):
                            ins = nc.tensor.transpose(dst[:, j * P:(j + 1) * P], src_[:, u % 4, j, :], identh[:, :])
                        ins.then_inc(S("att_pt_ps"), 1)

                def pv(u):
                    b = u // upb
                    if u % upb == 0 and b >= 1:
                        pe.wait_ge(S("att_att"), past(c, "att") + b)
                    pe.wait_ge(S("att_pt"), past(c, "pt") + u + 1)
                    pe.wait_ge(S("att_ptl"), past(c, "ptl") + u + 1)
                    for j, (h, _, _, _) in enumerate(unit_heads(c, u)):
                        o_ = PS[:, 6, h * (dv + 1):(h + 1) * (dv + 1)]
                        hi = PTh[:, u % 2, 0, j * P:(j + 1) * P]
                        lo = PTh[:, u % 2, 1, j * P:(j + 1) * P]
                        vh, vl = V[0][:, b, kv_head(c, h), :], V[1][:, b, kv_head(c, h), :]
                        mm(o_, hi, vh, True, False)
                        mm(o_, hi, vl, False, False)
                        ins = mm(o_, lo, vh, False, True)
                    ins.then_inc(S("att_pv"), 1)

                U = upb * B
                pe.wait_ge(S("att_vf"), past(c, "vf") + B)
                pe.wait_ge(S("att_ones"), past(c, "ones") + 1)
                if cross:
                    pe.wait_ge(S("xmask"), 1)
                for u in range(U + 8):
                    if u < U:
                        scores(u)
                    if 0 <= u - 3 < U:
                        transposes(u - 3)
                    if u == 4:
                        pe.wait_ge(S("att_v"), past(c, "v") + B)
                    if 0 <= u - 4 < U:
                        pv(u - 4)
                    f = u - 6
                    if 0 <= f < U and f % upb == upb - 1:
                        b = f // upb
                        pe.wait_ge(S("att_att"), past(c, "att") + b + 1)
                        if b >= 1:
                            pe.wait_ge(S("x_updated"), stage * B + b)
                        for cc in range(DC):
                            ins = tr(PS[:, 7, cc * P:(cc + 1) * P], att[:, b % 2, cc * P:(cc + 1) * P])
                        ins.then_inc(S("att_attT_ps"), 1)
                    f = u - 7
                    if 0 <= f < U and f % upb == upb - 1:
                        b = f // upb
                        pe.wait_ge(S("att_attT"), past(c, "attT") + b + 1)
                        for cc in range(DC):
                            ins = mm(PS[:, 7, 256:512], attT[:, cc, :], WT[:, 3, cc, :], cc == 0, cc == 1)
                        ins.then_inc(S("att_proj"), 1)

            pe.wait_ge(S("const"), 4)
            attention(SELF0, 0)
            if stages < 2:
                return
            pe.wait_ge(S("ctx_loaded"), 16)
            for b in range(B):
                if b >= 2:
                    pe.wait_ge(S("ctxT_ready"), b - 1)
                for cc in range(DC):
                    ins = tr(PS[:, 4 + b % 2, cc * P:(cc + 1) * P], CT[:, b, cc * P:(cc + 1) * P])
                ins.then_inc(S("ctxT_ps"), 1)
            pe.wait_ge(S("ctxT_ready"), B)
            for b in range(B):
                pe.wait_ge(S("CR_ready"), b + 1)
                if b >= 2:
                    pe.wait_ge(S("ctxR_ready"), b - 1)
                for cc in range(DC):
                    ins = tr(PS[:, 4 + b % 2, cc * P:(cc + 1) * P], CR[:, b, cc * P:(cc + 1) * P])
                ins.then_inc(S("ctxR_ps"), 1)
            xnt(1)
            pe.wait_ge(S("const"), 6)
            pe.wait_ge(S("ctxR_ready"), B)
            for b in range(B):
                pe.wait_ge(S("ub"), b + 1)
                if b >= 2:
                    pe.wait_ge(S("wb_ready"), b - 1)
                mm(bank(4 + b % 2, 256), chgroup[:, :], ub[:, b, :], True, True).then_inc(S("skip_ps"), 1)
            pe.wait_ge(S("toe_loaded"), 16)
            for h in range(CH):
                for m in range(DC):
                    i = DC * h + m
                    if i >= 4:
                        pe.wait_ge(S("z"), i - 3)
                    pe.wait_ge(S("kv_ready"), i + 1)
                    for c in range(m + 1):
                        at = P - (m - c) * P
                        ins = mm(bank(i % 4), Toe[:, h, at:at + P], kv[:, h % 2, c, :], c == 0, c == m)
                    ins.then_inc(S("conv_done"), 1)
            pe.wait_ge(S("oT"), DC * CH)
            pe.wait_ge(S("xnT_ready"), 2 * B)
            for b in range(B):
                if b >= 2:
                    pe.wait_ge(S("x_updated"), B + b - 1)
                for m in range(DC):
                    ins = tr(PS[:, 6 + b % 2, m * P:(m + 1) * P], oT[:, m, b * P:(b + 1) * P])
                ins.then_inc(S("convT_ps"), 1)
            if stages < 3:
                return

            pe.wait_ge(S("b_e0"), 16 * 9)
            for cc in range(DC):
                tr(PS[:, 0, cc * NR:(cc + 1) * NR], cen_raw[:, cc * P:(cc + 1) * P])
            tr(PS[:, 0, 64:64 + NB0], b1row[:, :]).then_inc(S("small_e0_ps"), 1)
            xnt(2)
            pe.wait_ge(S("small_e0"), 2)
            pe.wait_ge(S("xnT_ready"), 3 * B)
            for b in range(B):
                for dc in range(DC):
                    ins = mm(PS[:, 2, b * NR:(b + 1) * NR], xnT[:, dc, b * P:(b + 1) * P], cenT[:, dc, :], dc == 0, dc == 1)
            ins.then_inc(S("score0_ps"), 1)
            pe.wait_ge(S("G3"), 1)
            for b in range(B):
                if b >= 2:
                    pe.wait_ge(S("g3T"), b - 1)
                tr(PS[0:96, b % 2, 0:P], G3[:, b, :])
                tr(PS[0:NE0, b % 2, P:2 * P], gf0[:, b, :]).then_inc(S("g3T_ps"), 1)
            pe.wait_ge(S("w_e0"), 16 * 9)
            pe.wait_ge(S("sel_ready"), 3)
            pe.wait_ge(S("g3T"), B)

            def up(i):
                half, blk = divmod(i, NB0)
                m = P if blk < NB0 - 1 else LAST0
                ts = slice(half * HF, (half + 1) * HF)
                if i >= 2:
                    pe.wait_ge(S("hid"), i - 1)
                for dc in range(DC):
                    ins = mm(bank(i % 2, parts=m), W1[:, dc, blk * P:blk * P + m], xnT[:, dc, ts], dc == 0, dc == 1)
                ins.then_inc(S("up0_ps"), 1)
                if i >= 2:
                    pe.wait_ge(S("hg"), i - 1)
                mm(bank(2 + i % 2, parts=m), sel[0:96, blk * P:blk * P + m], g3T[0:96, ts], True, True).then_inc(S("gate_ps"), 1)

            def down(i):
                half, blk = divmod(i, NB0)
                m = P if blk < NB0 - 1 else LAST0
                if blk == 0:
                    for t in range(4):
                        if half:
                            pe.wait_ge(S("x_updated"), 2 * B + t + 1)
                        b = 4 * half + t
                        mm(bank(4 + t, 256), g0T[:, b * P:(b + 1) * P], b2cat[:, :], True, False)
                pe.wait_ge(S("hg"), i + 1)
                for t in range(4):
                    ins = mm(bank(4 + t, 256), hg[0:m, i % 2, t * P:(t + 1) * P], W2[0:m, blk, :], False, blk == NB0 - 1)
                ins.then_inc(S("down0"), 1)

            n0 = NH * NB0
            up(0)
            for i in range(n0):
                if i + 1 < n0:
                    up(i + 1)
                down(i)
            if stages < 4:
                return
            attention(SELF1, 3)
            if stages < 5:
                return
            attention(CROSS, 4)
            if stages < 6:
                return

            pe.wait_ge(S("w_s1"), 48)
            pe.wait_ge(S("b_e1"), 32)
            for w in range(3):
                for ic in range(DC):
                    for oc in range(DC):
                        ins = tr(PS[:, w, ic * D + oc * P:ic * D + (oc + 1) * P], wraw[1][:, w, oc, ic * P:(ic + 1) * P])
                ins.then_inc(S("wt_ps_s1"), 1)
            for ic in range(DC):
                ins = tr(PS[:, 3, ic * E1:(ic + 1) * E1], rw_raw[:, ic * P:(ic + 1) * P])
            ins.then_inc(S("wt_ps_s1"), 1)
            pe.wait_ge(S("wt_s1"), 4)
            xnt(5)
            pe.wait_ge(S("xnT_ready"), 6 * B)
            for b in range(B):
                for dc in range(DC):
                    ins = mm(PS[:, 2, b * E1:(b + 1) * E1], xnT[:, dc, b * P:(b + 1) * P], rwT[:, dc, :], dc == 0, dc == 1)
            ins.then_inc(S("score1_ps"), 1)
            for j in range(NH * DC):
                half, ic = divmod(j, DC)
                ts = slice(half * HF, (half + 1) * HF)
                if j >= 2:
                    pe.wait_ge(S("s_up"), j - 1)
                for w in range(2):
                    for dc in range(DC):
                        ins = mm(bank(4 + 2 * (j % 2) + w), WT[:, w, dc, ic * P:(ic + 1) * P], xnT[:, dc, ts], dc == 0, dc == 1)
                ins.then_inc(S("s_ps"), 1)
            pe.wait_ge(S("selb1"), 1)
            pe.wait_ge(S("const"), 8)
            for b in range(B):
                o_ = PS[:, 3, b * E1:(b + 1) * E1]
                for b2 in range(b):
                    mm(o_, onesb[:, :], selb1[:, b2, :], b2 == 0, False)
                ins = mm(o_, before[:, :], selb1[:, b, :], b == 0, True)
            ins.then_inc(S("rank_ps"), 1)
            pe.wait_ge(S("s_up"), NH * DC)
            for b in range(B):
                pe.wait_ge(S("Pm"), b + 1)
                for part in range(3):
                    pe.wait_ge(S(("xs_hi", "xs_mid", "xs_lo")[part]), b + 1)
                    for k, (e0, e1) in enumerate(ESPAN):
                        for dc in range(DC):
                            ins = mm(bank(2 * k + dc, (e1 - e0) * CAP), xs[part][:, b, dc * P:(dc + 1) * P],
                                     Pm[:, b, e0 * CAP:e1 * CAP], b == 0 and part == 0, b == B - 1 and part == 2)
            ins.then_inc(S("gather_ps"), 1)
            pe.wait_ge(S("w3"), 1)
            for k in range(SC):
                for b in range(B):
                    ins = mm(PS[:, 6 + k // 5, k % 5 * 96:(k % 5 + 1) * 96], Pm[:, b, k * P:(k + 1) * P], w3[:, b, :],
                             b == 0, b == B - 1)
                if k % 5 == 4:
                    ins.then_inc(S("wslot_ps"), 1)

            def turn_onehots(k):
                if k < 2:
                    pe.wait_ge(S("wslot"), k + 1)
                else:
                    pe.wait_ge(S("PmT"), k - 1)
                o_ = PS[:, 6 + k % 2, :].bitcast(BF16)
                for b in range(B):
                    ins = nc.tensor.transpose(o_[:, b * P:(b + 1) * P], Pm[:, b, k * P:(k + 1) * P], identb[:, :])
                ins.then_inc(S("PmT_ps"), 1)

            def expert_up(gr):
                pe.wait_ge(S(f"ew{gr % 4}"), 16 * 3 * GE * (gr // 4 + 1))
                if gr >= 2:
                    pe.wait_ge(S("eh"), gr - 1)
                for q in range(GE):
                    e = GE * gr + q
                    for w in range(2):
                        for dc in range(DC):
                            ins = mm(PS[:, gr % 2, 256 * w + q * CAP:256 * w + (q + 1) * CAP],
                                     EW[:, e % WRING, w * D + dc * P:w * D + (dc + 1) * P],
                                     XpT[:, dc, e * CAP:(e + 1) * CAP], dc == 0, dc == 1)
                ins.then_inc(S("eup_ps"), 1)

            def expert_down(gr):
                pe.wait_ge(S("eh"), gr + 1)
                if gr >= 2:
                    pe.wait_ge(S("yT"), gr - 1)
                for q in range(GE):
                    e = GE * gr + q
                    for dc in range(DC):
                        ins = mm(PS[:, 2 + gr % 2, dc * GS + q * CAP:dc * GS + (q + 1) * CAP],
                                 EW[:, e % WRING, 2 * D + dc * P:2 * D + (dc + 1) * P],
                                 eh[:, gr % 4, q * CAP:(q + 1) * CAP], True, True)
                ins.then_inc(S("y_ps"), 1)

            pe.wait_ge(S("XpT_a"), 3)
            pe.wait_ge(S("XpT_v"), 3)
            expert_up(0)
            for gr in range(NGR):
                if gr + 1 < NGR:
                    expert_up(gr + 1)
                for k in ([gr] if gr < NGR - 1 else range(gr, SC)):
                    turn_onehots(k)
                expert_down(gr)
            pe.wait_ge(S("yT"), NGR)
            for k in range(0, SC, 2):
                if k >= 4:
                    pe.wait_ge(S("Yw"), k - 2)
                for kk in range(2):
                    for dc in range(DC):
                        ins = tr(PS[:, 4 + k // 2 % 2, kk * D + dc * P:kk * D + (dc + 1) * P],
                                 yT[:, dc, (k + kk) * P:(k + kk + 1) * P])
                ins.then_inc(S("Y_ps"), 1)
            pe.wait_ge(S("hs"), NH * DC)
            for b in range(B):
                if b >= 4:
                    pe.wait_ge(S("x_updated"), 5 * B + b - 3)
                o_ = bank(b % 4, D)
                for ic in range(DC):
                    mm(o_, hs[:, ic, b * P:(b + 1) * P], WT[:, 2, ic, :], ic == 0, False)
                for k in range(SC):
                    for part in range(3):
                        if b == 0:
                            pe.wait_ge(S(("y_hi", "y_mid", "y_lo")[part]), k + 1)
                        ins = mm(o_, PmT[:, k, b * P:(b + 1) * P], Y3[:, part, k, :], False, k == SC - 1 and part == 2)
                ins.then_inc(S("e1_out"), 1)


_INS = ['x', 'fside_S2_0', 'ctx_2048', 'mask_SxS2_bc0', 'mask_BxS2_bk0', 'L0_attn_Wq', 'L0_attn_Wk', 'L0_attn_Wv',
        'L0_attn_Wo', 'L0_attn_bo', 'L0_xattn_k', 'L0_ffn_shared_w1', 'L0_ffn_shared_b1', 'L0_ffn_shared_w2',
        'L0_ffn_shared_b2', 'L0_ffn_routed_w1', 'L0_ffn_routed_b1', 'L0_ffn_routed_w2', 'L0_ffn_routed_b2',
        'L0_ffn_centroids', 'L0_ffn_bias', 'L1_attn_Wq', 'L1_attn_bq', 'L1_attn_Wk', 'L1_attn_bk', 'L1_attn_Wv',
        'L1_attn_bv', 'L1_attn_Wo', 'L1_attn_bo', 'L1_xattn_Wq', 'L1_xattn_bq', 'L1_xattn_Wk', 'L1_xattn_bk',
        'L1_xattn_Wv', 'L1_xattn_bv', 'L1_xattn_Wo', 'L1_xattn_bo', 'L1_ffn_router_w', 'L1_ffn_e_bias',
        'L1_ffn_W_gate', 'L1_ffn_W_up', 'L1_ffn_W_down', 'L1_ffn_shared_gate', 'L1_ffn_shared_up',
        'L1_ffn_shared_down']


def kernel(**inputs):
    import numpy as _np
    import concourse.bacc as _bacc
    from concourse import mybir as _mybir
    from concourse.bass_utils import run_bass_kernel_spmd as _run

    nc = _bacc.Bacc("TRN2", target_bir_lowering=False, num_devices=1)
    arrays, args = {}, {}
    for name in _INS:
        a = _np.ascontiguousarray(inputs[name])
        arrays[f"in_{name}_dram"] = a
        args[name] = nc.dram_tensor(f"in_{name}_dram", a.shape, _mybir.dt.from_np(a.dtype), kind="ExternalInput").ap()
    out = nc.dram_tensor("out_0_dram", (B, P, D), _mybir.dt.float32, kind="ExternalOutput").ap()
    decoder_kernel(nc, args, out, stages=STAGES)
    r = _run(nc, [arrays], core_ids=[0])
    return r.results[0]["out_0_dram"]


STAGES = 6
```

```python
from contextlib import ExitStack

import concourse.bass as bass
from concourse import mybir
from concourse.alu_op_type import AluOpType as ALU

ACT = mybir.ActivationFunctionType
AX = mybir.AxisListType
F32 = mybir.dt.float32
BF16 = mybir.dt.bfloat16
F16 = mybir.dt.float16
U8 = mybir.dt.uint8

P = 128
B = 8
D = 256
DC = D // P
T = B * P
EPS = 1e-5
NEG = -1.0e30
FAR = -3.0e38
HF = 512
NH = T // HF

CH, CI = 16, 8

NS, NR, FF, KR = 2, 16, 176, 4
NE0 = NS + NR
F0 = NE0 * FF
NB0 = -(-F0 // P)
LAST0 = F0 - (NB0 - 1) * P
GROUP = 32

E1, I1, NG1, TKG, K1 = 32, 128, 8, 3, 4
CAP = -(-5 * T // (4 * E1))
SLOTS = E1 * CAP
SC = SLOTS // P
SCALE1 = 2.5
ESPAN = [(0, 11), (11, 22), (22, 32)]
WRING = 16


def decoder_kernel(nc, A, out):
    ctx = ExitStack()
    with ctx:
        def sb(name, shape, dt=F32):
            return ctx.enter_context(nc.sbuf_tensor(name, shape, dt))

        sems = {}

        def S(name):
            if name not in sems:
                sems[name] = ctx.enter_context(nc.semaphore(name))
            return sems[name]

        X = sb("X", [P, B, D])
        xn = sb("xn", [P, B, D])
        xnT = sb("xnT", [P, DC, T])
        CT = sb("CT", [P, B, D])
        ctxT = sb("ctxT", [P, DC, T])
        wraw = [sb(f"wraw{i}", [P, 4, DC, D]) for i in range(2)]
        WT = sb("WT", [P, 4, DC, D])
        ident = sb("ident", [P, P])
        identb = sb("identb", [P, P], BF16)
        identh = sb("identh", [P, P], F16)
        causal = sb("causal", [P, P], BF16)
        chgroup = sb("chgroup", [P, P])
        before = sb("before", [P, P], BF16)
        onesb = sb("onesb", [P, P], BF16)
        slot_iota = sb("slot_iota", [P, CAP])
        skip = sb("skip", [P, 1])
        bcol = sb("bcol", [P, 3, 4])
        bbc = sb("bbc", [P, 5, D])
        bias0 = sb("bias0", [P, NR])
        ebias = sb("ebias", [P, E1])
        stats = sb("stats", [P, B, 6])
        mv = sb("mv", [P, B, 2])
        rstd = sb("rstd", [P, B])
        veps = sb("veps", [P, B])
        mhalf = sb("mhalf", [P, 1])
        mx = sb("mx", [P, 2, 8])
        rec = sb("rec", [P, 2, 32])
        cen_raw = sb("cen_raw", [NR, D])
        cenT = sb("cenT", [P, DC, NR])
        rw_raw = sb("rw_raw", [E1, D])
        rwT = sb("rwT", [P, DC, E1])
        b1row = sb("b1row", [NB0, P])
        b1col = sb("b1col", [P, NB0])
        b2cat = sb("b2cat", [NE0, D])

        R1 = sb("R1", [P, DC * F0 + NB0 * D])
        W1 = R1[:, 0:DC * F0].rearrange("p (c f) -> p c f", c=DC)
        W2 = R1[:, DC * F0:DC * F0 + NB0 * D].rearrange("p (k d) -> p k d", k=NB0)
        EW = R1[:, 0:WRING * 3 * D].rearrange("p (e w) -> p e w", e=WRING)

        R2 = sb("R2", [P, 16384])
        pair = R2[:, 0:4096].bitcast(F16).rearrange("p (s c t) -> p s c t", s=4, c=DC)
        Ph = R2[:, 0:2048].bitcast(F16).rearrange("p (n h k) -> p n h k", n=4, h=8)
        Pl = R2[:, 2048:4096].bitcast(F16).rearrange("p (n h k) -> p n h k", n=4, h=8)
        QS = R2[:, 4096:8192].bitcast(F16).rearrange("p (g t) -> p g t", g=8)
        KSa = R1[:, 4096:8192].bitcast(F16).rearrange("p (g t) -> p g t", g=8)
        KSb = R2[:, 8192:12288].bitcast(F16).rearrange("p (g t) -> p g t", g=8)
        VH = R2[:, 12288:13376].bitcast(F16)
        VL = R2[:, 13376:14464].bitcast(F16)
        V16 = [v_.rearrange("p (b h e) -> p b h e", b=B, h=16) for v_ in (VH, VL)]
        V8 = [v_[:, 0:B * 72].rearrange("p (b h e) -> p b h e", b=B, h=8) for v_ in (VH, VL)]
        Toe = R2[:, 8192:12288].rearrange("p (h l) -> p h l", h=CH)
        xmask = R2[:, 14464:14464 + B * P // 2].bitcast(BF16).rearrange("p (b k) -> p b k", b=B)
        att = R2[:, 14976:14976 + 2 * D].rearrange("p (n d) -> p n d", n=2)
        vf = att
        attT = R2[:, 15488:15488 + D].rearrange("p (c t) -> p c t", c=DC)
        mk8 = R2[:, 15744:16000].bitcast(U8).rearrange("p (b k) -> p b k", b=B)
        mq8 = R2[:, 16000:16032].bitcast(U8)
        kv = R2[:, 0:2048].rearrange("p (n c t) -> p n c t", n=2, c=DC)
        kin = R1[0:CH, 0:D]
        krev = R1[0:CH, D:2 * D + P]
        zb = R2[:, 2048:4096].rearrange("p (n t) -> p n t", n=4)
        oT = R2[:, 4096:6144].rearrange("p (c t) -> p c t", c=DC)
        ub = R2[:, 6144:8192].rearrange("p (b d) -> p b d", b=B)
        wb = R2[:, 12288:14336].rearrange("p (b d) -> p b d", b=B)
        hid = R2[:, 0:1024].rearrange("p (n t) -> p n t", n=2)
        hg = R2[:, 1024:2048].rearrange("p (n t) -> p n t", n=2)
        xn16 = R2[:, 8192:10240].bitcast(F16).rearrange("p (n c t) -> p n c t", n=2, c=DC)
        w1s = R2[:, 10240:11264].bitcast(F16).rearrange("p (r n c f) -> p r n c f", r=4, n=2, c=DC)
        w2s = R2[:, 11264:12288].bitcast(F16).rearrange("p (r n d) -> p r n d", r=4, n=2)
        hg16 = R2[:, 12288:13824].bitcast(F16).rearrange("p (r n t) -> p r n t", r=3, n=2)
        sel = wraw[0][:, :, :, :].rearrange("p a c d -> p (a c d)")[:, 0:F0 // 2].bitcast(BF16)
        g0T = R2[0:NE0, 6800:6800 + T]
        g3T = R2[:, 3700:3700 + T // 2].bitcast(BF16)
        o = 4400
        sc0 = R2[:, o:o + B * 20].rearrange("p (b e) -> p b e", b=B)
        rp0 = R2[:, o + 160:o + 320].rearrange("p (b e) -> p b e", b=B)
        m80 = R2[:, o + 320:o + 384].rearrange("p (b e) -> p b e", b=B)
        gv0 = R2[:, o + 384:o + 512].rearrange("p (b e) -> p b e", b=B)
        gs0 = R2[:, o + 512:o + 520]
        gr0 = R2[:, o + 520:o + 528]
        G3 = R2[:, o + 528:o + 528 + B * 96].rearrange("p (b e) -> p b e", b=B)
        gb0 = R2[:, o + 1296:o + 1296 + B * 8].bitcast(BF16).rearrange("p (b e) -> p b e", b=B)
        gf0 = R2[:, o + 1400:o + 1400 + B * NE0].rearrange("p (b e) -> p b e", b=B)
        rs0 = R2[:, o + 1600:o + 1600 + B * 16].rearrange("p (b e) -> p b e", b=B)
        Pm = R2[:, 0:B * SLOTS // 2].bitcast(F16).rearrange("p (b s) -> p b s", b=B)
        PmT = R2[:, 5120:5120 + SC * T // 2].bitcast(F16).rearrange("p (k t) -> p k t", k=SC)
        Xp = R2[:, 10240:10240 + 2 * SLOTS].bitcast(F16).rearrange("p (n c s) -> p n c s", n=2, c=DC)
        yT = R2[:, 12800:12800 + 2 * SLOTS].rearrange("p (c s) -> p c s", c=DC)
        Y2 = R2[:, 0:SC * D].bitcast(F16).rearrange("p (n k d) -> p n k d", n=2, k=SC)
        w3 = R2[:, 15360:15360 + B * 48].bitcast(F16).rearrange("p (b e) -> p b e", b=B)
        slot_of = R2[:, 15744:15744 + SC * E1].rearrange("p (k e) -> p k e", k=SC)
        wslot = R2[:, 16064:16064 + SC]
        wr0 = wraw[0][:, :, :, :].rearrange("p a c d -> p (a c d)")
        rs1 = wr0[:, 0:256].rearrange("p (b e) -> p b e", b=B)
        sb1 = wr0[:, 256:512].rearrange("p (b e) -> p b e", b=B)
        mk1 = wr0[:, 512:512 + B * 36].rearrange("p (b e) -> p b e", b=B)
        rp1 = wr0[:, 800:800 + B * 36].rearrange("p (b e) -> p b e", b=B)
        gt1 = wr0[:, 1088:1344].rearrange("p (b e) -> p b e", b=B)
        vl1 = wr0[:, 1344:1600].rearrange("p (b e) -> p b e", b=B)
        gs1 = wr0[:, 1600:1600 + B * 13].rearrange("p (b e) -> p b e", b=B)
        gp1 = wr0[:, 1704:1704 + B * 13].rearrange("p (b e) -> p b e", b=B)
        m81 = wr0[:, 1808:1872].rearrange("p (b e) -> p b e", b=B)
        mg1 = wr0[:, 1872:1936].rearrange("p (b e) -> p b e", b=B)
        su1 = wr0[:, 1936:1944]
        rc1 = wr0[:, 1944:1952]
        Pb = sb("Pb", [P, 2, 8, P])
        PT = sb("PT", [P, 4, 4 * P])
        PTh = PT[:, :, :].rearrange("p a k -> p (a k)").bitcast(F16).rearrange("p (n s k) -> p n s k", n=2, s=2)

        xs = [PT[:, 2 * n:2 * n + 2, :].rearrange("p a k -> p (a k)").bitcast(F16).rearrange("p (b d) -> p b d", b=B)
              for n in range(2)]
        pb1 = Pb[:, 1, :, :].rearrange("p h k -> p (h k)")
        big1 = pb1[:, 0:128].rearrange("p (g a) -> p g a", a=2)
        small1 = pb1[:, 128:256].rearrange("p (g a) -> p g a", a=2)
        t1 = pb1[:, 256:320]
        t2 = pb1[:, 320:448].rearrange("p (g a) -> p g a", a=2)
        sel1 = pb1[:, 448:704].rearrange("p (b e) -> p b e", b=B)
        selb1 = pb1[:, 704:832].bitcast(BF16).rearrange("p (b e) -> p b e", b=B)
        gmask1 = pb1[:, 832:896].rearrange("p (b g) -> p b g", b=B)
        wtmp = vl1
        wprod = wr0[:, 0:480].rearrange("p (k s e) -> p k s e", k=5, s=3)
        gact = ctxT[:, 0, :].rearrange("p (n t) -> p n t", n=2)
        uact = ctxT[:, 1, :].rearrange("p (n t) -> p n t", n=2)
        hs = CT[:, :, :].rearrange("p b d -> p (b d)").rearrange("p (c t) -> p c t", c=DC)
        esig = xnT[:, 0, 0:640].rearrange("p (n s) -> p n s", n=4)
        ef = xnT[:, 1, 0:640].rearrange("p (n s) -> p n s", n=4)
        eh = xnT[:, 0, 640:960].bitcast(F16).rearrange("p (n a s) -> p n a s", n=2, a=2)

        def two_experts(t):
            return t[:, 0:2 * 3 * D].bitcast(F16).rearrange("p (e a w) -> p e a w", e=2, a=2)
        EW16 = [two_experts(t_) for t_ in (
            xn[:, :, :].rearrange("p b d -> p (b d)"),
            wraw[1][:, :, :, :].rearrange("p a c d -> p (a c d)"),
            ctxT[:, :, :].rearrange("p c t -> p (c t)"),
            Pb[:, :, :, :].rearrange("p a h k -> p (a h k)"),
            wr0,
            PT[:, :, :].rearrange("p a k -> p (a k)"))]

        ctxR = Pb[:, :, :, :].rearrange("p a h k -> p a (h k)")
        CR = PT[:, :, :].rearrange("p a k -> p (a k)").rearrange("p (b d) -> p b d", b=B)

        def backwards(t, n):
            last = t[:, P - 1:P]
            return bass.AP(last.tensor, last.offset, [last.ap[0], [P, n], [-1, P]])

        PS = ctx.enter_context(nc.psum_tensor("PS", [P, 8, 512], F32))

        def bank(i, n=512, parts=P):
            return PS[0:parts, i, 0:n]

        kscr = nc.dram_tensor("kscr", (CH, P + D), F32, kind="Internal").ap()

        qk_scr = [nc.dram_tensor(f"qk_scr{i}", (4, D, T), F16, kind="Internal").ap() for i in range(3)]

        out_v = out.rearrange("b t d -> t b d")

        SELF0 = dict(n="a0", H=16, dv=16, upb=2, raw=0, sc=0.25, qb=0, vb=None, ob=0, KS=KSa)
        SELF1 = dict(n="a1", H=16, dv=16, upb=2, raw=1, sc=0.25, qb=1, vb=1, ob=2, KS=KSb)
        CROSS = dict(n="ax", H=32, dv=8, upb=4, raw=0, sc=float(8.0 ** -0.5), qb=2, vb=3, ob=4, KS=KSb)
        ATTENTIONS = [SELF0, SELF1, CROSS]

        def past(c, event):
            total = 0
            for a in ATTENTIONS[:ATTENTIONS.index(c)]:
                units = a["upb"] * B
                total += {"wt": 4, "wt_ps": 4, "qk_ps": jobs(a), "qk_hi": jobs(a), "qk": jobs(a), "ones": 1,
                          "stacked": 16 * 12 * (2 if a is CROSS else 1), "parked": 16 * 4,
                          "s": units, "sub": units, "exph": units, "exp": units, "pl": units, "pv": units,
                          "pt": units, "ptl": units, "pt_ps": 2 * units}.get(event, B)
            return total

        def jobs(c):
            return NH * (3 if c is CROSS else 4)

        def job_list(c):
            one = [(0, 0), (0, 1), (1, 0)] + ([] if c is CROSS else [(1, 1)])
            return [(half, w, cc) for half in range(NH) for w, cc in one]

        def unit_heads(c, u):
            if c is CROSS:
                rp, gh = divmod(u % 4, 2)
                return [(4 * (4 * gh + j) + 2 * rp + k, 32 * (2 * rp + k), 24, 4 * gh + j)
                        for k in range(2) for j in range(4)]
            return [(8 * (u % 2) + 2 * j + k, 64 * k, 48, 4 * (u % 2) + j) for k in range(2) for j in range(4)]

        def kv_head(c, h):
            return h // 4 if c["n"] == "ax" else h

        TURN = [0, 2, 4, 0, 0, 0]
        GE = 4
        NGR = E1 // GE
        GS = GE * CAP

        block = ctx.enter_context(nc.Block())

        @block.sync
        def _(sp):
            tot = {}

            def load(dst, src, sem, **kw):
                tot[sem] = tot.get(sem, 0) + 16
                sp.dma_start(dst, src, **kw).then_inc(S(sem), 16)

            def load_w(i, slot, w, sem):
                tot[sem] = tot.get(sem, 0) + 16
                sp.dma_start(wraw[i][:, slot, :, :], w.rearrange("(c p) i -> p c i", p=P)).then_inc(S(sem), 16)

            for b in range(B):
                load(X[:, b, :], A["x"][b], f"x_loaded{b}")
            for j, w in enumerate("qkvo"):
                load_w(0, j, A[f"L0_attn_W{w}"], "w_a0")
            load(bbc[:, 0, :], A["L0_attn_bo"].partition_broadcast(P), "bo_a0")
            load(kin[:, :], A["L0_xattn_k"], "k_loaded")
            load(CT[:, :, :], A["ctx_2048"].rearrange("b t d -> t b d"), "ctx_loaded")
            sp.wait_ge(S("krev_ready"), 1)
            load(kscr, krev[:, :], "kscr_written")
            sp.wait_ge(S("kscr_written"), 16)
            load(Toe[:, :, :], bass.AP(kscr.tensor, 0, [[1, P], [P + D, CH], [1, D]]), "toe_loaded")
            load(skip[:, :], A["fside_S2_0"].rearrange("(p a) -> p a", a=1), "skip_loaded")
            load_w(1, 0, A["L1_attn_Wq"], "w_a1")
            for j, w in list(enumerate("qkvo"))[1:]:
                load_w(1, j, A[f"L1_attn_W{w}"], "w_a1")
            for j, (n, k) in enumerate([("attn", "q"), ("attn", "k")]):
                for cc in range(DC):
                    load(bcol[:, 1, 2 * j + cc:2 * j + cc + 1],
                         A[f"L1_{n}_b{k}"][cc * P:(cc + 1) * P].rearrange("(p a) -> p a", a=1), "b_a1")
            load(bbc[:, 1, :], A["L1_attn_bv"].partition_broadcast(P), "b_a1")
            load(bbc[:, 2, :], A["L1_attn_bo"].partition_broadcast(P), "b_a1")

            def stack(c):
                scr = qk_scr[ATTENTIONS.index(c)]
                dv = c["dv"]
                tiles = 4 if c is CROSS else 2
                pitch = P // tiles
                for half in range(NH):
                    ts = slice(half * HF, (half + 1) * HF)
                    sp.wait_ge(S(f"att_parked{half}"), past(c, "parked") + 64)
                    for tile in range(tiles):
                        for w, parts in ((0, (0, 0, 1)), (1, (2, 3, 2))):
                            for term, part in enumerate(parts):
                                row = pitch * tile + dv * term
                                if w == 1 and c is CROSS:
                                    src = scr[part, 0:64, ts].rearrange("(g d) t -> d g t", g=8)
                                else:
                                    src = scr[part, :, ts].rearrange("(g s d) t -> s d g t", g=8, s=tiles)[tile]
                                dst = (QS, c["KS"])[w]
                                sp.dma_start(dst[row:row + dv, :, ts], src).then_inc(S(f"att_stacked{half}"), 16)

            stack(SELF0)
            sp.wait_ge(S("att_s"), 2 * B)
            for c in range(DC):
                load(W1[:, c, 0:NS * FF].rearrange("p (n f) -> p n f", n=NS),
                     A["L0_ffn_shared_w1"][:, c * P:(c + 1) * P, :].rearrange("n p f -> p n f"), "w_e0")
                load(W1[:, c, NS * FF:F0].rearrange("p (n f) -> p n f", n=NR),
                     A["L0_ffn_routed_w1"][:, c * P:(c + 1) * P, :].rearrange("n p f -> p n f"), "w_e0")
            sw2 = A["L0_ffn_shared_w2"].rearrange("n f d -> (n f) d")
            rw2 = A["L0_ffn_routed_w2"].rearrange("n f d -> (n f) d")
            full = NS * FF // P
            rem = NS * FF - full * P
            mid = NB0 - 2 - full
            load(W2[:, 0:full, :], sw2[0:full * P].rearrange("(k p) d -> p k d", p=P), "w_e0")
            load(W2[0:rem, full, :], sw2[full * P:NS * FF], "w_e0")
            load(W2[rem:P, full, :], rw2[0:P - rem], "w_e0")
            load(W2[:, full + 1:full + 1 + mid, :],
                 rw2[P - rem:P - rem + mid * P].rearrange("(k p) d -> p k d", p=P), "w_e0")
            load(W2[0:LAST0, NB0 - 1, :], rw2[P - rem + mid * P:NR * FF], "w_e0")
            sp.wait_ge(S("b1row_cleared"), 1)
            sb1 = A["L0_ffn_shared_b1"].rearrange("n f -> (n f)")
            rb1 = A["L0_ffn_routed_b1"].rearrange("n f -> (n f)")

            def row(v):
                return v.rearrange("(a f) -> a f", a=1)
            load(b1row[0:full, :], sb1[0:full * P].rearrange("(k p) -> k p", p=P), "b_e0")
            load(b1row[full:full + 1, 0:rem], row(sb1[full * P:NS * FF]), "b_e0")
            load(b1row[full:full + 1, rem:P], row(rb1[0:P - rem]), "b_e0")
            load(b1row[full + 1:full + 1 + mid, :],
                 rb1[P - rem:P - rem + mid * P].rearrange("(k p) -> k p", p=P), "b_e0")
            load(b1row[NB0 - 1:NB0, 0:LAST0], row(rb1[P - rem + mid * P:NR * FF]), "b_e0")
            load(b2cat[0:NS, :], A["L0_ffn_shared_b2"], "b_e0")
            load(b2cat[NS:NE0, :], A["L0_ffn_routed_b2"], "b_e0")
            load(cen_raw[:, :], A["L0_ffn_centroids"], "b_e0")
            load(bias0[:, :], A["L0_ffn_bias"].partition_broadcast(P), "b_e0")
            for cc in range(DC):
                load(bcol[:, 2, cc:cc + 1], A["L1_xattn_bq"][cc * P:(cc + 1) * P].rearrange("(p a) -> p a", a=1), "b_ax")
            load(bcol[0:64, 2, 2:3], A["L1_xattn_bk"].rearrange("(p a) -> p a", a=1), "b_ax")
            load(bbc[:, 3, 0:64], A["L1_xattn_bv"].partition_broadcast(P), "b_ax")
            load(bbc[:, 4, :], A["L1_xattn_bo"].partition_broadcast(P), "b_ax")
            load(mq8[:, :], A["mask_SxS2_bc0"], "b_ax")
            load(mk8[:, :, :], A["mask_BxS2_bk0"].partition_broadcast(P), "b_ax")
            sp.wait_ge(S("x_updated"), 3 * B)
            load_w(0, 0, A["L1_xattn_Wq"], "w_ax")
            load(wraw[0][0:64, 1, 0, :], A["L1_xattn_Wk"], "w_ax")
            load(wraw[0][0:64, 2, 0, :], A["L1_xattn_Wv"], "w_ax")
            load_w(0, 3, A["L1_xattn_Wo"], "w_ax")
            load(rw_raw[:, :], A["L1_ffn_router_w"], "b_e1")
            load(ebias[:, :], A["L1_ffn_e_bias"].partition_broadcast(P), "b_e1")
            stack(SELF1)
            sp.wait_ge(S("att_wt"), 8)
            load_w(1, 0, A["L1_ffn_shared_gate"], "w_s1")
            load_w(1, 1, A["L1_ffn_shared_up"], "w_s1")
            load_w(1, 2, A["L1_ffn_shared_down"], "w_s1")
            for e in range(E1):
                if e == WRING:
                    stack(CROSS)
                if e >= WRING and e % GE == 0:
                    sp.wait_ge(S("cwA_lo"), (e - WRING) // GE + 1)
                    sp.wait_ge(S("cwB_lo"), (e - WRING) // GE + 1)
                sl = e % WRING
                for k, w in enumerate(("W_gate", "W_up")):
                    load(EW[:, sl, k * D:(k + 1) * D].rearrange("p (c i) -> p c i", c=DC),
                         A[f"L1_ffn_{w}"][e].rearrange("(c p) i -> p c i", p=P), f"ew{sl // GE}")
                load(EW[:, sl, 2 * D:3 * D], A["L1_ffn_W_down"][e], f"ew{sl // GE}")
            for b in range(B):
                sp.wait_ge(S("x_updated"), 5 * B + b + 1)
                sp.dma_start(out_v[:, b, :], X[:, b, :]).then_inc(S("stored"), 16)
            sp.wait_ge(S("stored"), 16 * B)

        @block.gpsimd
        def _(pool):
            chain = [0]

            def link(ins):
                chain[0] += 1
                ins.then_inc(S("pool_chain"), 1)
                pool.wait_ge(S("pool_chain"), chain[0])

            g = nc.gpsimd
            link(g.memset(krev[:, D:D + P], 0.0))
            pool.wait_ge(S("k_loaded"), 16)
            g.tensor_copy(krev[:, 0:D], bass.AP(kin[:, D - 1:D].tensor, kin[:, D - 1:D].offset,
                                                [kin[:, D - 1:D].ap[0], [-1, D]])).then_inc(S("krev_ready"), 1)
            link(g.memset(mhalf[:, :], -0.5))

            def rstd_of(stage, b):
                pool.wait_ge(S("var_ready"), stage * B + b + 1)
                link(g.tensor_scalar(veps[:, b:b + 1], mv[:, b, 1:2], EPS, None, ALU.add))
                g.tensor_tensor(rstd[:, b:b + 1], veps[:, b:b + 1], mhalf[:, :],
                                ALU.pow).then_inc(S("rstd_ready"), 1)

            def rstds(stage, then=None, first=0):
                for b in range(B + 1):
                    if first <= b < B:
                        rstd_of(stage, b)
                    if b >= 1 and then:
                        then(b - 1)

            def band(t, v, lo, hi, pattern, mult=1, fill0=1.0):
                link(g.memset(v, 1.0))
                link(g.affine_select(out=v, in_=v, compare_op=ALU.is_ge, fill=0.0, base=lo,
                                     pattern=pattern, channel_multiplier=mult))
                return g.affine_select(out=v, in_=v, compare_op=ALU.is_ge, fill=0.0, base=hi,
                                       pattern=[[-s, n] for s, n in pattern], channel_multiplier=-mult)

            link(g.memset(ident[:, :], 0.0))
            g.affine_select(out=ident[:, :], in_=ident[:, :], compare_op=ALU.not_equal, fill=1.0, base=0,
                            pattern=[[-1, P]], channel_multiplier=1).then_inc(S("const"), 1)
            link(g.memset(identb[:, :], 0.0))
            g.affine_select(out=identb[:, :], in_=identb[:, :], compare_op=ALU.not_equal, fill=1.0, base=0,
                            pattern=[[-1, P]], channel_multiplier=1).then_inc(S("const"), 1)
            pool.wait_ge(S("const"), 1)
            link(g.memset(causal[:, :], 0.0))
            g.affine_select(out=causal[:, :], in_=causal[:, :], compare_op=ALU.is_ge, fill=NEG, base=0,
                            pattern=[[-1, P]], channel_multiplier=1).then_inc(S("const"), 1)
            g.tensor_copy(identh[:, :], ident[:, :]).then_inc(S("const"), 1)
            g.memset(bcol[:, 0, :], 0.0).then_inc(S("const"), 1)
            band(chgroup, chgroup[:, :].rearrange("p (a i) -> p a i", a=CH), 0, CI - 1,
                 [[-CI, CH], [0, CI]]).then_inc(S("const"), 1)
            link(g.memset(onesb[:, :], 1.0))
            g.affine_select(out=before[:, :], in_=onesb[:, :], compare_op=ALU.is_ge, fill=0.0, base=-1,
                            pattern=[[1, P]], channel_multiplier=-1).then_inc(S("const"), 1)
            g.iota(slot_iota[:, :], pattern=[[1, CAP]], base=-1000, channel_multiplier=0,
                   allow_small_or_imprecise_dtypes=True).then_inc(S("const"), 1)

            def add_row(c, stage, b):
                sem, n = ("bo_a0", 16) if c["n"] == "a0" else ("b_a1", 96) if c["n"] == "a1" else ("b_ax", 16 * 7)
                pool.wait_ge(S(sem), n)
                pool.wait_ge(S("ln_done"), stage * B + b + 1)
                g.tensor_tensor(X[:, b, :], X[:, b, :], bbc[:, c["ob"], :], ALU.add).then_inc(S("x_biased"), 1)

            def low_parts(c, next_stage, then=None):
                cross = c is CROSS
                V, nkv, dv = (V8, 8, 8) if cross else (V16, 16, 16)
                for b in range(B):
                    pool.wait_ge(S("att_vh"), past(c, "vh") + b + 1)
                    g.tensor_tensor(V[1][:, b, :, 0:dv], vf[:, b % 2, 0:nkv * dv].rearrange("p (h e) -> p h e", h=nkv),
                                    V[0][:, b, :, 0:dv], ALU.subtract).then_inc(S("att_v"), 1)
                upb = c["upb"]
                U = upb * B
                for u in range(U + 9):
                    if u < U:
                        pool.wait_ge(S("att_exp"), past(c, "exp") + u + 1)
                        if u >= 4:
                            pool.wait_ge(S("att_pt_ps"), past(c, "pt_ps") + 2 * (u - 3))
                        g.tensor_tensor(Pl[:, u % 4, :, :], Pb[:, u % 2, :, :], Ph[:, u % 4, :, :],
                                        ALU.subtract).then_inc(S("att_pl"), 1)
                    if 0 <= u - 7 < U and (u - 7) % upb == upb - 1:
                        rstd_of(next_stage, (u - 7) // upb)
                    if 0 <= u - 9 < U and (u - 9) % upb == upb - 1 and then:
                        then((u - 9) // upb)

            rstds(0, lambda b: add_row(SELF0, 0, b))
            pool.wait_ge(S("att_wt"), 4)
            def selector(part):
                band(sel, sel[part * GROUP:(part + 1) * GROUP, :], 0, FF - 1, [[1, F0]],
                     mult=-FF).then_inc(S("sel_ready"), 1)
                pool.wait_ge(S("sel_ready"), part + 1)

            selector(0)
            selector(1)
            low_parts(SELF0, 1)
            pool.wait_ge(S("ctx_loaded"), 16)
            pool.wait_ge(S("att_pv"), past(SELF1, "pv"))
            for b in range(B):
                g.tensor_copy(CR[:, b, :].rearrange("p (c l) -> p c l", c=DC), backwards(CT[:, b, :], DC)).then_inc(S("CR_ready"), 1)
            pool.wait_ge(S("xnT_ready"), 2 * B)
            pool.wait_ge(S("ctxT_ready"), B)
            for h in range(CH):
                if h >= 2:
                    pool.wait_ge(S("conv_done"), 2 * (h - 1))
                for m in range(DC):
                    v = xnT[:, m, :].rearrange("p (b c) -> p b c", b=B)[:, :, h * CI:(h + 1) * CI]
                    k = ctxT[:, m, :].rearrange("p (b c) -> p b c", b=B)[:, :, h * CI:(h + 1) * CI]
                    g.tensor_tensor(kv[:, h % 2, m, :].rearrange("p (b i j) -> p b i j", b=B, i=CI),
                                    v.unsqueeze(3).broadcast_to([P, B, CI, CI]),
                                    k.unsqueeze(2).broadcast_to([P, B, CI, CI]),
                                    ALU.mult).then_inc(S("kv_ready"), 1)
            for b in range(B):
                pool.wait_ge(S("wb_ready"), b + 1)
                g.tensor_tensor(X[:, b, :], X[:, b, :], wb[:, b, :], ALU.add).then_inc(S("x_skip"), 1)
            def flat(b):
                pool.wait_ge(S("ln_done"), 2 * B + b + 1)
                g.tensor_tensor(X[:, b, :], X[:, b, :], xn[:, b, :], ALU.add).then_inc(S("x_flat"), 1)
            rstds(2, flat)
            for half in range(NH):
                pool.wait_ge(S("xn16_hi"), half + 1)
                ts = slice(half * HF, (half + 1) * HF)
                pool.wait_ge(S("x_flat"), B)
                g.tensor_tensor(xn16[:, 1, :, ts], xnT[:, :, ts], xn16[:, 0, :, ts], ALU.subtract).then_inc(S("xn16_lo"), 1)
            pool.wait_ge(S("xn16_lo"), NH)
            selector(2)
            for i in range(NH * NB0):
                blk = i % NB0
                m = P if blk < NB0 - 1 else LAST0
                pool.wait_ge(S("w16_hi"), 2 * i + 2)
                g.tensor_tensor(w1s[:, i % 4, 1, :, 0:m], W1[:, :, blk * P:blk * P + m], w1s[:, i % 4, 0, :, 0:m],
                                ALU.subtract).then_inc(S("w16_lo"), 1)
                g.tensor_tensor(w2s[0:m, i % 4, 1, :], W2[0:m, blk, :], w2s[0:m, i % 4, 0, :],
                                ALU.subtract).then_inc(S("w16_lo"), 1)
                if i == NB0 + 2:
                    for b in range(B // NH):
                        rstd_of(3, b)
            rstds(3, lambda b: add_row(SELF1, 3, b), first=B // NH)
            low_parts(SELF1, 4, lambda b: add_row(CROSS, 4, b))
            low_parts(CROSS, 5)
            pool.wait_ge(S("att_proj"), 3 * B)
            band(slot_of, slot_of, 0, CAP - 1, [[P, SC], [-CAP, E1]]).then_inc(S("slot_of"), 1)
            for b in range(B):
                pool.wait_ge(S("xs_hi"), b + 1)
                g.tensor_tensor(xs[1][:, b, :], xn[:, b, :], xs[0][:, b, :], ALU.subtract).then_inc(S("xs_lo"), 1)
            for j in range(NH * DC):
                half, ic = divmod(j, DC)
                pool.wait_ge(S("s_up"), j + 1)
                g.tensor_tensor(hs[:, ic, half * HF:(half + 1) * HF], gact[:, j % 2, :], uact[:, j % 2, :],
                                ALU.mult).then_inc(S("hs"), 1)
            for gr in range(NGR):
                pool.wait_ge(S("cwB_hi"), gr + 1)
                w = EW16[2 * (gr % 3) + 1]
                e = GE * gr % WRING + 2
                g.tensor_tensor(w[:, :, 1, :], EW[:, e:e + 2, :], w[:, :, 0, :], ALU.subtract).then_inc(S("cwB_lo"), 1)

        @block.scalar
        def _(act):
            s = nc.scalar
            chain = [0]

            def link(ins):
                chain[0] += 1
                ins.then_inc(S("act_chain"), 1)
                act.wait_ge(S("act_chain"), chain[0])

            def xnt(stage):
                for b in range(B):
                    act.wait_ge(S("xnT_ps"), stage * B + b + 1)
                    s.activation(xnT[:, :, b * P:(b + 1) * P],
                                 bank(TURN[stage] + b % 2, 256).rearrange("p (c t) -> p c t", c=DC),
                                 ACT.Copy).then_inc(S("xnT_ready"), 1)

            def weights(c):
                n = c["n"]
                for w in range(4):
                    act.wait_ge(S("att_wt_ps"), past(c, "wt_ps") + w + 1)
                    src = bank(w).rearrange("p (c o) -> p c o", c=DC)
                    if n != "ax" or w in (0, 3):
                        s.activation(WT[:, w, :, :], src, ACT.Copy).then_inc(S("att_wt"), 1)
                    else:
                        s.activation(WT[:, w, :, 0:64], src[:, :, 0:64], ACT.Copy).then_inc(S("att_wt"), 1)

            def park(c, half):
                scr = qk_scr[ATTENTIONS.index(c)]
                ts = slice(half * HF, (half + 1) * HF)
                act.wait_ge(S("att_qk_hi"), past(c, "qk_hi") + (half + 1) * jobs(c) // NH)
                act.wait_ge(S("att_qk"), past(c, "qk") + (half + 1) * jobs(c) // NH)
                for part in range(4):
                    if c is CROSS and part >= 2:
                        act.dma_start(scr[part, 0:64, ts], pair[0:64, part, 0, ts]).then_inc(S(f"att_parked{half}"), 16)
                    else:
                        act.dma_start(scr[part, :, ts].rearrange("(c p) t -> p c t", p=P),
                                      pair[:, part, :, ts]).then_inc(S(f"att_parked{half}"), 16)

            def attention(c, stage):
                n, H, dv, upb = c["n"], c["H"], c["dv"], c["upb"]
                cross = n == "ax"
                weights(c)
                xnt(stage)
                if c is SELF0:
                    act.wait_ge(S("const"), 5)
                else:
                    act.wait_ge(S(f"b_{n}"), 96 if n == "a1" else 16 * 7)
                for i, (half, w, cc) in enumerate(job_list(c)):
                    m = 64 if cross and w else P
                    act.wait_ge(S("att_qk_ps"), past(c, "qk_ps") + i + 1)
                    s.activation(pair[0:m, 2 * w, cc, half * HF:(half + 1) * HF], bank(i % 4, parts=m), ACT.Identity,
                                 bias=bcol[0:m, c["qb"], 2 * w + cc:2 * w + cc + 1]).then_inc(S("att_qk_hi"), 1)
                    if i == jobs(c) // NH:
                        park(c, 0)
                park(c, 1)
                V, nkv = (V8, 8) if cross else (V16, 16)
                for b in range(B):
                    act.wait_ge(S("att_vf"), past(c, "vf") + b + 1)
                    s.activation(V[0][:, b, :, 0:dv], vf[:, b % 2, 0:nkv * dv].rearrange("p (h e) -> p h e", h=nkv),
                                 ACT.Copy).then_inc(S("att_vh"), 1)
                U = upb * B
                for half in range(NH):
                    act.wait_ge(S(f"att_parked{half}"), past(c, "parked") + 64)
                for u in range(U + 8):
                    t = u - 3
                    if 0 <= t < U:
                        if t >= 2:
                            act.wait_ge(S("att_pv"), past(c, "pv") + t - 1)
                        act.wait_ge(S("att_pt_ps"), past(c, "pt_ps") + 2 * t + 2)
                        s.activation(PTh[:, t % 2, 1, :], PS[:, 5, :].bitcast(F16), ACT.Copy).then_inc(S("att_ptl"), 1)
                    if u < U:
                        act.wait_ge(S("att_sub"), past(c, "sub") + u + 1)
                        if u >= 4:
                            act.wait_ge(S("att_pt_ps"), past(c, "pt_ps") + 2 * (u - 3) - 1)
                        s.activation(Ph[:, u % 4, :, :], Pb[:, u % 2, :, :], ACT.Exp, scale=c["sc"]).then_inc(S("att_exph"), 1)
                        act.wait_ge(S("att_exph"), past(c, "exph") + u + 1)
                        s.activation(Pb[:, u % 2, :, :], Pb[:, u % 2, :, :], ACT.Exp, scale=c["sc"]).then_inc(S("att_exp"), 1)
                    f = u - 6
                    if f >= 0 and f < U and f % upb == upb - 1:
                        act.wait_ge(S("att_attT_ps"), past(c, "attT_ps") + f // upb + 1)
                        s.activation(attT[:, :, :], bank(7, 256).rearrange("p (c t) -> p c t", c=DC),
                                     ACT.Copy).then_inc(S("att_attT"), 1)

            attention(SELF0, 0)
            for b in range(B):
                act.wait_ge(S("ctxT_ps"), b + 1)
                s.activation(ctxT[:, :, b * P:(b + 1) * P], bank(4 + b % 2, 256).rearrange("p (c t) -> p c t", c=DC),
                             ACT.Copy).then_inc(S("ctxT_ready"), 1)
            for b in range(B):
                act.wait_ge(S("ctxR_ps"), b + 1)
                s.activation(ctxR[:, :, b * P:(b + 1) * P], bank(4 + b % 2, 256).rearrange("p (c t) -> p c t", c=DC),
                             ACT.Copy).then_inc(S("ctxR_ready"), 1)
            xnt(1)
            act.wait_ge(S("small_e0_ps"), 1)
            s.activation(cenT[:, :, :], bank(0, 32).rearrange("p (c e) -> p c e", c=DC), ACT.Copy).then_inc(S("small_e0"), 1)
            s.activation(b1col[:, :], PS[:, 0, 64:64 + NB0], ACT.Copy).then_inc(S("small_e0"), 1)
            xnt(2)
            for half in range(NH):
                act.wait_ge(S("xnT_ready"), 2 * B + (half + 1) * B // NH)
                ts = slice(half * HF, (half + 1) * HF)
                s.activation(xn16[:, 0, :, ts], xnT[:, :, ts], ACT.Copy).then_inc(S("xn16_hi"), 1)
            act.wait_ge(S("score0_ps"), 1)
            s.activation(rs0, bank(2, B * NR).rearrange("p (b e) -> p b e", b=B), ACT.Sigmoid).then_inc(S("score0"), 1)
            for b in range(B):
                act.wait_ge(S("g3T_ps"), b + 1)
                link(s.activation(g3T[0:96, b * P:(b + 1) * P], PS[0:96, b % 2, 0:P], ACT.Copy))
                s.activation(g0T[:, b * P:(b + 1) * P], PS[0:NE0, b % 2, P:2 * P], ACT.Copy).then_inc(S("g3T"), 1)

            def block_high(i):
                blk = i % NB0
                m = P if blk < NB0 - 1 else LAST0
                if i >= 4:
                    act.wait_ge(S("down0"), i - 3)
                s.activation(w1s[:, i % 4, 0, :, 0:m], W1[:, :, blk * P:blk * P + m], ACT.Copy).then_inc(S("w16_hi"), 1)
                s.activation(w2s[0:m, i % 4, 0, :], W2[0:m, blk, :], ACT.Copy).then_inc(S("w16_hi"), 1)

            act.wait_ge(S("w_e0"), 16 * 9)
            for i in range(3):
                block_high(i)
            for i in range(NH * NB0):
                blk = i % NB0
                m = P if blk < NB0 - 1 else LAST0
                if i >= 1 and i + 2 < NH * NB0:
                    block_high(i + 2)
                act.wait_ge(S("up0_ps"), i + 1)
                if i >= 2:
                    act.wait_ge(S("hg"), i - 1)
                s.activation(hid[0:m, i % 2, :], bank(i % 2, parts=m), ACT.Relu,
                             bias=b1col[0:m, blk:blk + 1]).then_inc(S("hid"), 1)
            attention(SELF1, 3)
            attention(CROSS, 4)
            for w in range(3):
                act.wait_ge(S("wt_ps_s1"), w + 1)
                s.activation(WT[:, w, :, :], bank(w).rearrange("p (c o) -> p c o", c=DC), ACT.Copy).then_inc(S("wt_s1"), 1)
            act.wait_ge(S("wt_ps_s1"), 4)
            s.activation(rwT[:, :, :], bank(3, 2 * E1).rearrange("p (c e) -> p c e", c=DC), ACT.Copy).then_inc(S("wt_s1"), 1)
            xnt(5)
            act.wait_ge(S("score1_ps"), 1)
            s.activation(rs1, bank(2, B * E1).rearrange("p (b e) -> p b e", b=B), ACT.Sigmoid).then_inc(S("score1"), 1)
            for b in range(B):
                s.activation(xs[0][:, b, :], xn[:, b, :], ACT.Copy).then_inc(S("xs_hi"), 1)

            def shared(j):
                act.wait_ge(S("s_ps"), j + 1)
                if j >= 2:
                    act.wait_ge(S("hs"), j - 1)
                s.activation(gact[:, j % 2, :], bank(4 + 2 * (j % 2)), ACT.Silu).then_inc(S("s_gate"), 1)
                s.activation(uact[:, j % 2, :], bank(5 + 2 * (j % 2)), ACT.Copy).then_inc(S("s_up"), 1)

            def high_parts(gr):
                act.wait_ge(S(f"ew{gr % 4}"), 16 * 3 * GE * (gr // 4 + 1))
                if gr == 0:
                    act.wait_ge(S("xs_lo"), B)
                elif gr == 1:
                    act.wait_ge(S("hs"), NH * DC)
                elif gr == 2:
                    act.wait_ge(S("wslot"), 2)
                else:
                    act.wait_ge(S("y_ps"), gr - 2)
                e = GE * gr % WRING
                s.activation(EW16[2 * (gr % 3)][:, :, 0, :], EW[:, e:e + 2, :], ACT.Copy).then_inc(S("cwA_hi"), 1)

            for j in range(NH * DC):
                shared(j)
            high_parts(0)
            high_parts(1)
            act.wait_ge(S("gather_ps"), 1)
            for k, (e0, e1) in enumerate(ESPAN):
                for dc in range(DC):
                    s.activation(Xp[:, 0, dc, e0 * CAP:e1 * CAP], bank(2 * k + dc, (e1 - e0) * CAP),
                                 ACT.Copy).then_inc(S("Xp_hi"), 1)
            for gr in range(NGR):
                act.wait_ge(S("eup_ps"), gr + 1)
                s.activation(esig[:, gr % 4, :], bank(gr % 2, GS), ACT.Silu).then_inc(S("esig"), 1)
                for k in ([gr] if gr < NGR - 1 else range(gr, SC)):
                    act.wait_ge(S("PmT_ps"), k + 1)
                    s.activation(PmT[:, k, :], PS[:, 6 + k % 2, :].bitcast(F16), ACT.Copy).then_inc(S("PmT"), 1)
                if gr + 2 < NGR:
                    high_parts(gr + 2)
            for k in range(SC):
                act.wait_ge(S("Y_ps"), k + 1)
                s.activation(Y2[:, 0, k, :], bank(4 + k % 4, D), ACT.Copy,
                             scale=wslot[:, k:k + 1]).then_inc(S("y_hi"), 1)

        @block.vector
        def _(dve):
            v = nc.vector
            chain = [0]

            def link(ins):
                chain[0] += 1
                ins.then_inc(S("dve_chain"), 1)
                dve.wait_ge(S("dve_chain"), chain[0])

            pending = []

            def variance(b):
                link(v.bn_stats(stats[:, b, :], X[:, b, :]))
                v.bn_aggr(mv[:, b, :], stats[:, b, :]).then_inc(S("var_ready"), 1)
                pending.append(b)

            def normalize():
                while pending:
                    b = pending.pop(0)
                    rstds_seen[0] += 1
                    dve.wait_ge(S("rstd_ready"), rstds_seen[0])
                    v.tensor_scalar(xn[:, b, :], X[:, b, :], mv[:, b, 0:1], rstd[:, b:b + 1], ALU.subtract,
                                    ALU.mult).then_inc(S("ln_done"), 1)

            rstds_seen = [0]

            def update(b, stage, src):
                x = X[:, b, :]
                if len(src.shape) == 3:
                    x = x.rearrange("p (c l) -> p c l", c=DC)
                v.tensor_tensor(x, x, src, ALU.add).then_inc(S("x_updated"), 1)
                if stage < 5:
                    dve.wait_ge(S("x_updated"), stage * B + b + 1)
                    variance(b)

            v.memset(b1row[:, :], 0.0).then_inc(S("b1row_cleared"), 1)
            for b in range(B):
                dve.wait_ge(S(f"x_loaded{b}"), 16)
                variance(b)
                if b >= 1:
                    first = pending.pop()
                    normalize()
                    pending.append(first)
            normalize()

            def attention(c, stage):
                n, H, dv, upb = c["n"], c["H"], c["dv"], c["upb"]
                cross = n == "ax"
                V, nkv = (V8, 8) if cross else (V16, 16)
                v.memset(V[0][:, :, :, dv:dv + 1], 1.0)
                v.memset(V[1][:, :, :, dv:dv + 1], 0.0).then_inc(S("att_ones"), 1)
                if n == "a1":
                    dve.wait_ge(S("b_a1"), 96)
                if cross:
                    dve.wait_ge(S("b_ax"), 16 * 7)
                    link(v.tensor_tensor(xmask[:, :, :], mk8[:, :, :],
                                         mq8[:, :].unsqueeze(1).broadcast_to([P, B, P]), ALU.max))
                    v.tensor_scalar(xmask[:, :, :], xmask[:, :, :], NEG, None, ALU.mult).then_inc(S("xmask"), 1)
                for i, (half, w, cc) in enumerate(job_list(c)):
                    m = 64 if cross and w else P
                    ts = slice(half * HF, (half + 1) * HF)
                    dve.wait_ge(S("att_qk_hi"), past(c, "qk_hi") + i + 1)
                    v.scalar_tensor_tensor(pair[0:m, 2 * w + 1, cc, ts], bank(i % 4, parts=m),
                                           bcol[0:m, c["qb"], 2 * w + cc:2 * w + cc + 1],
                                           pair[0:m, 2 * w, cc, ts], ALU.add, ALU.subtract).then_inc(S("att_qk"), 1)
                for b in range(B):
                    dve.wait_ge(S("att_v_ps"), past(c, "v_ps") + b + 1)
                    if b >= 2:
                        dve.wait_ge(S("att_v"), past(c, "v") + b - 1)
                    if c["vb"] is None:
                        v.tensor_copy(vf[:, b % 2, :], bank(4 + b % 2, nkv * dv)).then_inc(S("att_vf"), 1)
                    else:
                        v.tensor_tensor(vf[:, b % 2, 0:nkv * dv], bank(4 + b % 2, nkv * dv), bbc[:, c["vb"], 0:nkv * dv],
                                        ALU.add).then_inc(S("att_vf"), 1)
                U = upb * B
                for u in range(U + 8):
                    f = u - 5
                    if 0 <= f < U and f % upb == upb - 1:
                        b = f // upb
                        o = bank(6, H * (dv + 1)).rearrange("p (h e) -> p h e", h=H)
                        dve.wait_ge(S("att_pv"), past(c, "pv") + f + 1)
                        link(v.reciprocal(rec[:, b % 2, 0:H], o[:, :, dv]))
                        v.tensor_tensor(att[:, b % 2, :].rearrange("p (h e) -> p h e", h=H), o[:, :, 0:dv],
                                        rec[:, b % 2, 0:H].unsqueeze(2).broadcast_to([P, H, dv]),
                                        ALU.mult).then_inc(S("att_att"), 1)
                    if u < U:
                        sc = PS[:, 2 * (u % 2):2 * (u % 2) + 2, :].rearrange("p a (h k) -> p (a h) k", h=4)
                        dve.wait_ge(S("att_s"), past(c, "s") + u + 1)
                        link(v.tensor_reduce(mx[:, u % 2, :], sc, AX.X, ALU.max))
                        if u >= 2:
                            dve.wait_ge(S("att_pl"), past(c, "pl") + u - 1)
                        v.tensor_tensor(Pb[:, u % 2, :, :], sc, mx[:, u % 2, :].unsqueeze(2).broadcast_to([P, 8, P]),
                                        ALU.subtract).then_inc(S("att_sub"), 1)
                    t = u - 3
                    if 0 <= t < U:
                        if t >= 2:
                            dve.wait_ge(S("att_pv"), past(c, "pv") + t - 1)
                        dve.wait_ge(S("att_pt_ps"), past(c, "pt_ps") + 2 * t + 1)
                        v.tensor_copy(PTh[:, t % 2, 0, :], PS[:, 4, :].bitcast(F16)).then_inc(S("att_pt"), 1)
                    normalize()
                    f = u - 7
                    if 0 <= f < U and f % upb == upb - 1:
                        b = f // upb
                        dve.wait_ge(S("att_proj"), past(c, "proj") + b + 1)
                        dve.wait_ge(S("x_biased"), [0, 0, 0, 1, 2][stage] * B + b + 1)
                        update(b, stage, PS[:, 7, 256:512])
                normalize()

            attention(SELF0, 0)
            dve.wait_ge(S("ctx_loaded"), 16)
            dve.wait_ge(S("skip_loaded"), 16)
            dve.wait_ge(S("ln_done"), 2 * B)
            for b in range(B):
                v.scalar_tensor_tensor(ub[:, b, :], xn[:, b, :], skip[:, 0:1], CT[:, b, :], ALU.mult,
                                       ALU.mult).then_inc(S("ub"), 1)
            for b in range(B):
                dve.wait_ge(S("skip_ps"), b + 1)
                v.tensor_tensor(wb[:, b, :], CT[:, b, :], bank(4 + b % 2, 256), ALU.mult).then_inc(S("wb_ready"), 1)
            for h in range(CH):
                for m in range(DC):
                    i = DC * h + m
                    dve.wait_ge(S("conv_done"), i + 1)
                    x1 = ctxR[:, m, :].rearrange("p (b c) -> p b c", b=B)[:, :, h * CI:(h + 1) * CI]
                    z = zb[:, i % 4, :].rearrange("p (b i j) -> p b i j", b=B, i=CI)
                    v.tensor_tensor(z, bank(i % 4).rearrange("p (b i j) -> p b i j", b=B, i=CI),
                                    x1.unsqueeze(3).broadcast_to([P, B, CI, CI]), ALU.mult).then_inc(S("z"), 1)
                    dve.wait_ge(S("z"), i + 1)
                    v.tensor_reduce(oT[:, m, :].rearrange("p (b c) -> p b c", b=B)[:, :, h * CI:(h + 1) * CI],
                                    z.rearrange("p b i j -> p b j i"), AX.X, ALU.add).then_inc(S("oT"), 1)
            for b in range(B):
                dve.wait_ge(S("convT_ps"), b + 1)
                dve.wait_ge(S("x_skip"), b + 1)
                normalize()
                update(b, 1, backwards(bank(6 + b % 2, 256), DC))
            normalize()

            dve.wait_ge(S("b_e0"), 16 * 9)
            v.memset(sc0[:, :, NR:20], NEG).then_inc(S("pad0"), 1)
            link(v.memset(G3[:, :, :], 0.0))
            dve.wait_ge(S("score0"), 1)
            link(v.tensor_tensor(sc0[:, :, 0:NR], rs0, bias0[:, :].unsqueeze(1).broadcast_to([P, B, NR]), ALU.add))
            for b in range(B):
                ins = v.max(m80[:, b, :], sc0[:, b, 0:NR])
            link(ins)
            link(v.memset(m80[:, :, KR:8], NEG))
            dve.wait_ge(S("pad0"), 1)
            for b in range(B):
                ins = v.match_replace(out=rp0[:, b, :], in_to_replace=m80[:, b, :], in_values=sc0[:, b, :], imm_value=FAR)
            link(ins)
            link(v.tensor_tensor(gv0, rp0[:, :, 0:NR], sc0[:, :, 0:NR], ALU.not_equal))
            link(v.tensor_tensor(gv0, gv0, sc0[:, :, 0:NR], ALU.mult))
            link(v.tensor_reduce(gs0, gv0, AX.X, ALU.add))
            link(v.tensor_scalar(gs0, gs0, 1e-8, None, ALU.max))
            link(v.reciprocal(gr0, gs0))
            link(v.memset(gf0[:, :, 0:NS], 1.0))
            link(v.tensor_tensor(gf0[:, :, NS:NE0], gv0, gr0.unsqueeze(2).broadcast_to([P, B, NR]), ALU.mult))
            link(v.memset(G3[:, :, 0:NS], 1.0))
            for part in range(3):
                lo = part * GROUP + NS
                link(v.tensor_copy(gb0, gf0[:, :, NS:NE0] if part == 0 else gv0))
                link(v.tensor_copy(G3[:, :, lo:lo + NR], gb0))
                if part < 2:
                    link(v.tensor_tensor(gv0, gf0[:, :, NS:NE0] if part == 0 else gv0, gb0, ALU.subtract))
            v.tensor_copy(m80[:, 0, 0:1], m80[:, 0, 1:2]).then_inc(S("G3"), 1)
            for i in range(NH * NB0):
                m = P if i % NB0 < NB0 - 1 else LAST0
                dve.wait_ge(S("hid"), i + 1)
                dve.wait_ge(S("gate_ps"), i + 1)
                v.tensor_tensor(hg[0:m, i % 2, :], hid[0:m, i % 2, :], bank(2 + i % 2, parts=m),
                                ALU.mult).then_inc(S("hg"), 1)
                if i >= 3:
                    dve.wait_ge(S("down0"), i - 2)
                dve.wait_ge(S("hg"), i + 1)
                link(v.tensor_copy(hg16[0:m, i % 3, 0, :], hg[0:m, i % 2, :]))
                v.tensor_tensor(hg16[0:m, i % 3, 1, :], hg[0:m, i % 2, :], hg16[0:m, i % 3, 0, :],
                                ALU.subtract).then_inc(S("hg16"), 1)
                if i % NB0 == NB0 - 1:
                    half = i // NB0
                    dve.wait_ge(S("down0"), i + 1)
                    for t in range(4):
                        b = 4 * half + t
                        dve.wait_ge(S("x_flat"), b + 1)
                        normalize()
                        update(b, 2, bank(4 + t, 256))
            normalize()
            attention(SELF1, 3)
            attention(CROSS, 4)

            dve.wait_ge(S("b_e1"), 32)
            v.memset(gs1[:, :, NG1:13], NEG)
            link(v.memset(mk1[:, :, E1:36], NEG))
            dve.wait_ge(S("score1"), 1)
            link(v.tensor_tensor(sb1, rs1, ebias[:, :].unsqueeze(1).broadcast_to([P, B, E1]), ALU.add))
            pairs = sb1.rearrange("p b e -> p (b e)").rearrange("p (g a c) -> p g a c", a=2, c=2)
            v.tensor_reduce(big1, pairs, AX.X, ALU.max)
            link(v.tensor_reduce(small1, pairs, AX.X, ALU.min))
            v.tensor_tensor(t1, big1[:, :, 0], big1[:, :, 1], ALU.add)
            link(v.tensor_tensor(t2, big1, small1, ALU.add))
            link(v.tensor_tensor(t2[:, :, 0], t2[:, :, 0], t2[:, :, 1], ALU.max))
            link(v.tensor_tensor(gs1[:, :, 0:NG1], t2[:, :, 0].rearrange("p (b g) -> p b g", b=B),
                                 t1.rearrange("p (b g) -> p b g", b=B), ALU.max))
            for b in range(B):
                ins = v.max(mg1[:, b, :], gs1[:, b, 0:NG1])
            link(ins)
            link(v.memset(mg1[:, :, TKG:8], NEG))
            for b in range(B):
                ins = v.match_replace(out=gp1[:, b, :], in_to_replace=mg1[:, b, :], in_values=gs1[:, b, :], imm_value=FAR)
            link(ins)
            link(v.tensor_tensor(gmask1, gp1[:, :, 0:NG1], gs1[:, :, 0:NG1], ALU.not_equal))
            link(v.tensor_tensor(mk1[:, :, 0:E1].rearrange("p b (g k) -> p b g k", g=NG1),
                                 sb1.rearrange("p b (g k) -> p b g k", g=NG1),
                                 gmask1.unsqueeze(3).broadcast_to([P, B, NG1, E1 // NG1]), ALU.mult))
            for b in range(B):
                ins = v.max(m81[:, b, :], mk1[:, b, 0:E1])
            link(ins)
            link(v.memset(m81[:, :, K1:8], NEG))
            for b in range(B):
                ins = v.match_replace(out=rp1[:, b, :], in_to_replace=m81[:, b, :], in_values=mk1[:, b, :], imm_value=FAR)
            link(ins)
            link(v.tensor_tensor(sel1, rp1[:, :, 0:E1], mk1[:, :, 0:E1], ALU.not_equal))
            v.tensor_copy(selb1, sel1).then_inc(S("selb1"), 1)
            link(v.tensor_tensor(gt1, sel1, rs1, ALU.mult))
            link(v.tensor_reduce(su1, gt1, AX.X, ALU.add))
            link(v.tensor_scalar(su1, su1, 1e-20, None, ALU.add))
            link(v.reciprocal(rc1, su1))
            link(v.tensor_tensor(gt1, gt1, rc1.unsqueeze(2).broadcast_to([P, B, E1]), ALU.mult))
            link(v.tensor_scalar(gt1, gt1, SCALE1, None, ALU.mult))
            dve.wait_ge(S("rank_ps"), 1)
            link(v.scalar_tensor_tensor(vl1.rearrange("p b e -> p (b e)"), sel1.rearrange("p b e -> p (b e)"), -1000.0,
                                        bank(3, B * E1), ALU.mult, ALU.add))
            dve.wait_ge(S("att_proj"), 3 * B)
            for b in range(B):
                v.tensor_tensor(Pm[:, b, :].rearrange("p (e c) -> p e c", e=E1),
                                vl1[:, b, :].unsqueeze(2).broadcast_to([P, E1, CAP]),
                                slot_iota[:, :].unsqueeze(1).broadcast_to([P, E1, CAP]),
                                ALU.is_equal).then_inc(S("Pm"), 1)
            dve.wait_ge(S("Pm"), B)
            for part in range(3):
                link(v.tensor_copy(w3[:, :, part * E1:(part + 1) * E1], gt1))
                if part < 2:
                    link(v.tensor_tensor(gt1, gt1, w3[:, :, part * E1:(part + 1) * E1], ALU.subtract))
            v.memset(su1, 0.0).then_inc(S("w3"), 1)

            def split_weights(gr):
                dve.wait_ge(S(f"ew{gr % 4}"), 16 * 3 * GE * (gr // 4 + 1))
                if gr == 0:
                    dve.wait_ge(S("wt_s1"), 4)
                elif gr >= 3:
                    dve.wait_ge(S("y_ps"), gr - 2)
                e = GE * gr % WRING
                v.tensor_copy(EW16[2 * (gr % 3) + 1][:, :, 0, :], EW[:, e + 2:e + 4, :]).then_inc(S("cwB_hi"), 1)
                w = EW16[2 * (gr % 3)]
                dve.wait_ge(S("cwA_hi"), gr + 1)
                v.tensor_tensor(w[:, :, 1, :], EW[:, e:e + 2, :], w[:, :, 0, :], ALU.subtract).then_inc(S("cwA_lo"), 1)

            split_weights(0)
            split_weights(1)
            dve.wait_ge(S("gather_ps"), 1)
            for k, (e0, e1) in enumerate(ESPAN):
                for dc in range(DC):
                    dve.wait_ge(S("Xp_hi"), DC * k + dc + 1)
                    v.tensor_tensor(Xp[:, 1, dc, e0 * CAP:e1 * CAP], bank(2 * k + dc, (e1 - e0) * CAP),
                                    Xp[:, 0, dc, e0 * CAP:e1 * CAP], ALU.subtract).then_inc(S("Xp_lo"), 1)
            dve.wait_ge(S("slot_of"), 1)
            for hb in range(2):
                dve.wait_ge(S("wslot_ps"), hb + 1)
                for k in range(5):
                    ins = v.tensor_tensor(wprod[:, k, :, :],
                                          PS[:, 6 + hb, k * 96:(k + 1) * 96].rearrange("p (s e) -> p s e", s=3),
                                          slot_of[:, 5 * hb + k, :].unsqueeze(1).broadcast_to([P, 3, E1]), ALU.mult)
                link(ins)
                v.tensor_reduce(wslot[:, 5 * hb:5 * hb + 5], wprod, AX.XY, ALU.add).then_inc(S("wslot"), 1)
                dve.wait_ge(S("wslot"), hb + 1)
            for gr in range(NGR):
                dve.wait_ge(S("esig"), gr + 1)
                link(v.tensor_tensor(ef[:, gr % 4, :], esig[:, gr % 4, :], PS[:, gr % 2, 256:256 + GS], ALU.mult))
                link(v.tensor_copy(eh[:, gr % 2, 0, :], ef[:, gr % 4, :]))
                v.tensor_tensor(eh[:, gr % 2, 1, :], ef[:, gr % 4, :], eh[:, gr % 2, 0, :],
                                ALU.subtract).then_inc(S("eh"), 1)
                if gr >= 1:
                    k = gr - 1
                    dve.wait_ge(S("y_ps"), k + 1)
                    v.tensor_copy(yT[:, :, k * GS:(k + 1) * GS], PS[:, 2 + k % 2, 0:2 * GS].rearrange("p (c s) -> p c s", c=DC)).then_inc(S("yT"), 1)
                if gr + 2 < NGR:
                    split_weights(gr + 2)
            k = NGR - 1
            dve.wait_ge(S("y_ps"), k + 1)
            v.tensor_copy(yT[:, :, k * GS:(k + 1) * GS], PS[:, 2 + k % 2, 0:2 * GS].rearrange("p (c s) -> p c s", c=DC)).then_inc(S("yT"), 1)
            for k in range(SC):
                dve.wait_ge(S("y_hi"), k + 1)
                v.scalar_tensor_tensor(Y2[:, 1, k, :], bank(4 + k % 4, D), wslot[:, k:k + 1],
                                       Y2[:, 0, k, :], ALU.mult, ALU.subtract).then_inc(S("y_lo"), 1)
            for b in range(B):
                dve.wait_ge(S("e1_out"), b + 1)
                update(b, 5, bank(b % 4, 256))

        @block.tensor
        def _(pe):
            PRODUCTS = ((0, 0), (0, 1), (1, 0))

            def mm(o_, l, r, start, stop):
                return nc.tensor.matmul(o_, l, r, start=start, stop=stop)

            def tr(o_, i_):
                k = i_.shape[0]
                return nc.tensor.transpose(o_, i_, ident[0:k, 0:k])

            def xnt(stage):
                for b in range(B):
                    pe.wait_ge(S("ln_done"), stage * B + b + 1)
                    i = stage * B + b
                    if b >= 2:
                        pe.wait_ge(S("xnT_ready"), i - 1)
                    for cc in range(DC):
                        ins = tr(PS[:, TURN[stage] + b % 2, cc * P:(cc + 1) * P], xn[:, b, cc * P:(cc + 1) * P])
                    ins.then_inc(S("xnT_ps"), 1)

            def weights(c):
                n, raw = c["n"], wraw[c["raw"]]
                pe.wait_ge(S(f"w_{n}"), 64)
                for w in range(4):
                    rows = 64 if n == "ax" and w in (1, 2) else D
                    for ic in range(DC):
                        for oc in range(-(-rows // P)):
                            k = min(P, rows - oc * P)
                            ins = tr(PS[:, w, ic * D + oc * P:ic * D + oc * P + k],
                                     raw[0:k, w, oc, ic * P:(ic + 1) * P])
                    ins.then_inc(S("att_wt_ps"), 1)

            def attention(c, stage):
                n, H, dv, upb = c["n"], c["H"], c["dv"], c["upb"]
                cross = n == "ax"
                V = V8 if cross else V16
                weights(c)
                pe.wait_ge(S("att_wt"), past(c, "wt") + 4)
                xnt(stage)
                src = ctxT if cross else xnT
                pe.wait_ge(S("xnT_ready"), stage * B + B)
                for i, (half, w, cc) in enumerate(job_list(c)):
                    m = 64 if cross and w else P
                    if i >= 4:
                        pe.wait_ge(S("att_qk"), past(c, "qk") + i - 3)
                    for dc in range(DC):
                        ins = mm(bank(i % 4, parts=m), WT[:, w, dc, cc * P:cc * P + m],
                                 (src if w else xnT)[:, dc, half * HF:(half + 1) * HF], dc == 0, dc == 1)
                    ins.then_inc(S("att_qk_ps"), 1)
                for b in range(B):
                    if b >= 2:
                        pe.wait_ge(S("att_vf"), past(c, "vf") + b - 1)
                    w = 64 if cross else D
                    for dc in range(DC):
                        ins = mm(bank(4 + b % 2, w), src[:, dc, b * P:(b + 1) * P], WT[:, 2, dc, 0:w], dc == 0, dc == 1)
                    ins.then_inc(S("att_v_ps"), 1)

                per_half = 384 if cross else 192

                def scores(u):
                    b = u // upb
                    if u % (upb * B // NH) == 0:
                        pe.wait_ge(S(f"att_stacked{u // (upb * B // NH)}"), past(c, "stacked") + per_half)
                    if u >= 2:
                        pe.wait_ge(S("att_sub"), past(c, "sub") + u - 1)
                    p0 = 2 * (u % 2)
                    mask = xmask[:, b, :] if cross else causal[:, :]
                    for k in range(2):
                        mm(bank(p0 + k), identb[:, :], mask.unsqueeze(1).broadcast_to([P, 4, P]), True, False)
                    ts = slice(b * P, (b + 1) * P)
                    for j in range(4):
                        for k in range(2):
                            _, row, rows, idx = unit_heads(c, u)[4 * k + j]
                            ins = mm(PS[:, p0 + k, j * P:(j + 1) * P], QS[row:row + rows, idx, ts],
                                     c["KS"][row:row + rows, idx, ts], False, j == 3)
                    ins.then_inc(S("att_s"), 1)

                def transposes(u):
                    for k, src_ in ((0, Ph), (1, Pl)):
                        pe.wait_ge(S(("att_exph", "att_pl")[k]), past(c, ("exph", "pl")[k]) + u + 1)
                        if u >= 1:
                            pe.wait_ge(S(("att_pt", "att_ptl")[k]), past(c, ("pt", "ptl")[k]) + u)
                        dst = PS[:, 4 + k, :].bitcast(F16)
                        for j in range(8):
                            ins = nc.tensor.transpose(dst[:, j * P:(j + 1) * P], src_[:, u % 4, j, :], identh[:, :])
                        ins.then_inc(S("att_pt_ps"), 1)

                def pv(u):
                    b = u // upb
                    if u % upb == 0 and b >= 1:
                        pe.wait_ge(S("att_att"), past(c, "att") + b)
                    pe.wait_ge(S("att_pt"), past(c, "pt") + u + 1)
                    pe.wait_ge(S("att_ptl"), past(c, "ptl") + u + 1)
                    for j, (h, _, _, _) in enumerate(unit_heads(c, u)):
                        o_ = PS[:, 6, h * (dv + 1):(h + 1) * (dv + 1)]
                        hi = PTh[:, u % 2, 0, j * P:(j + 1) * P]
                        lo = PTh[:, u % 2, 1, j * P:(j + 1) * P]
                        vh, vl = V[0][:, b, kv_head(c, h), :], V[1][:, b, kv_head(c, h), :]
                        mm(o_, hi, vh, True, False)
                        mm(o_, hi, vl, False, False)
                        ins = mm(o_, lo, vh, False, True)
                    ins.then_inc(S("att_pv"), 1)

                U = upb * B
                pe.wait_ge(S("att_vf"), past(c, "vf") + B)
                pe.wait_ge(S("att_ones"), past(c, "ones") + 1)
                if cross:
                    pe.wait_ge(S("xmask"), 1)
                for u in range(U + 8):
                    if u < U:
                        scores(u)
                    if 0 <= u - 3 < U:
                        transposes(u - 3)
                    if u == 4:
                        pe.wait_ge(S("att_v"), past(c, "v") + B)
                    if 0 <= u - 4 < U:
                        pv(u - 4)
                    f = u - 6
                    if 0 <= f < U and f % upb == upb - 1:
                        b = f // upb
                        pe.wait_ge(S("att_att"), past(c, "att") + b + 1)
                        if b >= 1:
                            pe.wait_ge(S("x_updated"), stage * B + b)
                        for cc in range(DC):
                            ins = tr(PS[:, 7, cc * P:(cc + 1) * P], att[:, b % 2, cc * P:(cc + 1) * P])
                        ins.then_inc(S("att_attT_ps"), 1)
                    f = u - 7
                    if 0 <= f < U and f % upb == upb - 1:
                        b = f // upb
                        pe.wait_ge(S("att_attT"), past(c, "attT") + b + 1)
                        for cc in range(DC):
                            ins = mm(PS[:, 7, 256:512], attT[:, cc, :], WT[:, 3, cc, :], cc == 0, cc == 1)
                        ins.then_inc(S("att_proj"), 1)

            pe.wait_ge(S("const"), 4)
            attention(SELF0, 0)
            pe.wait_ge(S("ctx_loaded"), 16)
            for b in range(B):
                if b >= 2:
                    pe.wait_ge(S("ctxT_ready"), b - 1)
                for cc in range(DC):
                    ins = tr(PS[:, 4 + b % 2, cc * P:(cc + 1) * P], CT[:, b, cc * P:(cc + 1) * P])
                ins.then_inc(S("ctxT_ps"), 1)
            pe.wait_ge(S("ctxT_ready"), B)
            for b in range(B):
                pe.wait_ge(S("CR_ready"), b + 1)
                if b >= 2:
                    pe.wait_ge(S("ctxR_ready"), b - 1)
                for cc in range(DC):
                    ins = tr(PS[:, 4 + b % 2, cc * P:(cc + 1) * P], CR[:, b, cc * P:(cc + 1) * P])
                ins.then_inc(S("ctxR_ps"), 1)
            xnt(1)
            pe.wait_ge(S("const"), 6)
            pe.wait_ge(S("ctxR_ready"), B)
            for b in range(B):
                pe.wait_ge(S("ub"), b + 1)
                if b >= 2:
                    pe.wait_ge(S("wb_ready"), b - 1)
                mm(bank(4 + b % 2, 256), chgroup[:, :], ub[:, b, :], True, True).then_inc(S("skip_ps"), 1)
            pe.wait_ge(S("toe_loaded"), 16)
            for h in range(CH):
                for m in range(DC):
                    i = DC * h + m
                    if i >= 4:
                        pe.wait_ge(S("z"), i - 3)
                    pe.wait_ge(S("kv_ready"), i + 1)
                    for c in range(m + 1):
                        at = P - (m - c) * P
                        ins = mm(bank(i % 4), Toe[:, h, at:at + P], kv[:, h % 2, c, :], c == 0, c == m)
                    ins.then_inc(S("conv_done"), 1)
            pe.wait_ge(S("oT"), DC * CH)
            pe.wait_ge(S("xnT_ready"), 2 * B)
            for b in range(B):
                if b >= 2:
                    pe.wait_ge(S("x_updated"), B + b - 1)
                for m in range(DC):
                    ins = tr(PS[:, 6 + b % 2, m * P:(m + 1) * P], oT[:, m, b * P:(b + 1) * P])
                ins.then_inc(S("convT_ps"), 1)

            pe.wait_ge(S("b_e0"), 16 * 9)
            for cc in range(DC):
                tr(PS[:, 0, cc * NR:(cc + 1) * NR], cen_raw[:, cc * P:(cc + 1) * P])
            tr(PS[:, 0, 64:64 + NB0], b1row[:, :]).then_inc(S("small_e0_ps"), 1)
            xnt(2)
            pe.wait_ge(S("small_e0"), 2)
            pe.wait_ge(S("xnT_ready"), 3 * B)
            for b in range(B):
                for dc in range(DC):
                    ins = mm(PS[:, 2, b * NR:(b + 1) * NR], xnT[:, dc, b * P:(b + 1) * P], cenT[:, dc, :], dc == 0, dc == 1)
            ins.then_inc(S("score0_ps"), 1)
            pe.wait_ge(S("G3"), 1)
            for b in range(B):
                if b >= 2:
                    pe.wait_ge(S("g3T"), b - 1)
                tr(PS[0:96, b % 2, 0:P], G3[:, b, :])
                tr(PS[0:NE0, b % 2, P:2 * P], gf0[:, b, :]).then_inc(S("g3T_ps"), 1)
            pe.wait_ge(S("w_e0"), 16 * 9)
            pe.wait_ge(S("sel_ready"), 3)
            pe.wait_ge(S("xn16_lo"), NH)
            pe.wait_ge(S("g3T"), B)

            def up(i):
                half, blk = divmod(i, NB0)
                m = P if blk < NB0 - 1 else LAST0
                ts = slice(half * HF, (half + 1) * HF)
                if i >= 2:
                    pe.wait_ge(S("hid"), i - 1)
                pe.wait_ge(S("w16_lo"), 2 * i + 2)
                for dc in range(DC):
                    for pw, px in PRODUCTS:
                        ins = mm(bank(i % 2, parts=m), w1s[:, i % 4, pw, dc, 0:m], xn16[:, px, dc, ts],
                                 dc == 0 and pw + px == 0, dc == 1 and pw == 1)
                ins.then_inc(S("up0_ps"), 1)
                if i >= 2:
                    pe.wait_ge(S("hg"), i - 1)
                mm(bank(2 + i % 2, parts=m), sel[0:96, blk * P:blk * P + m], g3T[0:96, ts], True, True).then_inc(S("gate_ps"), 1)

            def down(i):
                half, blk = divmod(i, NB0)
                m = P if blk < NB0 - 1 else LAST0
                if blk == 0:
                    for t in range(4):
                        if half:
                            pe.wait_ge(S("x_updated"), 2 * B + t + 1)
                        b = 4 * half + t
                        mm(bank(4 + t, 256), g0T[:, b * P:(b + 1) * P], b2cat[:, :], True, False)
                pe.wait_ge(S("hg16"), i + 1)
                for t in range(4):
                    for pw, ph in PRODUCTS:
                        ins = mm(bank(4 + t, 256), hg16[0:m, i % 3, ph, t * P:(t + 1) * P], w2s[0:m, i % 4, pw, :],
                                 False, blk == NB0 - 1 and pw == 1)
                ins.then_inc(S("down0"), 1)

            n0 = NH * NB0
            up(0)
            up(1)
            for i in range(n0):
                if i + 2 < n0:
                    up(i + 2)
                down(i)
            attention(SELF1, 3)
            attention(CROSS, 4)

            pe.wait_ge(S("w_s1"), 48)
            pe.wait_ge(S("b_e1"), 32)
            for w in range(3):
                for ic in range(DC):
                    for oc in range(DC):
                        ins = tr(PS[:, w, ic * D + oc * P:ic * D + (oc + 1) * P], wraw[1][:, w, oc, ic * P:(ic + 1) * P])
                ins.then_inc(S("wt_ps_s1"), 1)
            for ic in range(DC):
                ins = tr(PS[:, 3, ic * E1:(ic + 1) * E1], rw_raw[:, ic * P:(ic + 1) * P])
            ins.then_inc(S("wt_ps_s1"), 1)
            pe.wait_ge(S("wt_s1"), 4)
            xnt(5)
            pe.wait_ge(S("xnT_ready"), 6 * B)
            for b in range(B):
                for dc in range(DC):
                    ins = mm(PS[:, 2, b * E1:(b + 1) * E1], xnT[:, dc, b * P:(b + 1) * P], rwT[:, dc, :], dc == 0, dc == 1)
            ins.then_inc(S("score1_ps"), 1)
            for j in range(NH * DC):
                half, ic = divmod(j, DC)
                ts = slice(half * HF, (half + 1) * HF)
                if j >= 2:
                    pe.wait_ge(S("s_up"), j - 1)
                for w in range(2):
                    for dc in range(DC):
                        ins = mm(bank(4 + 2 * (j % 2) + w), WT[:, w, dc, ic * P:(ic + 1) * P], xnT[:, dc, ts], dc == 0, dc == 1)
                ins.then_inc(S("s_ps"), 1)
            pe.wait_ge(S("selb1"), 1)
            pe.wait_ge(S("const"), 8)
            for b in range(B):
                o_ = PS[:, 3, b * E1:(b + 1) * E1]
                for b2 in range(b):
                    mm(o_, onesb[:, :], selb1[:, b2, :], b2 == 0, False)
                ins = mm(o_, before[:, :], selb1[:, b, :], b == 0, True)
            ins.then_inc(S("rank_ps"), 1)
            pe.wait_ge(S("s_up"), NH * DC)
            for b in range(B):
                pe.wait_ge(S("Pm"), b + 1)
                for part in range(2):
                    pe.wait_ge(S(("xs_hi", "xs_lo")[part]), b + 1)
                    for k, (e0, e1) in enumerate(ESPAN):
                        for dc in range(DC):
                            ins = mm(bank(2 * k + dc, (e1 - e0) * CAP), xs[part][:, b, dc * P:(dc + 1) * P],
                                     Pm[:, b, e0 * CAP:e1 * CAP], b == 0 and part == 0, b == B - 1 and part == 1)
            ins.then_inc(S("gather_ps"), 1)
            pe.wait_ge(S("w3"), 1)
            for k in range(SC):
                for b in range(B):
                    ins = mm(PS[:, 6 + k // 5, k % 5 * 96:(k % 5 + 1) * 96], Pm[:, b, k * P:(k + 1) * P], w3[:, b, :],
                             b == 0, b == B - 1)
                if k % 5 == 4:
                    ins.then_inc(S("wslot_ps"), 1)

            def turn_onehots(k):
                if k < 2:
                    pe.wait_ge(S("wslot"), k + 1)
                else:
                    pe.wait_ge(S("PmT"), k - 1)
                o_ = PS[:, 6 + k % 2, :].bitcast(F16)
                for b in range(B):
                    ins = nc.tensor.transpose(o_[:, b * P:(b + 1) * P], Pm[:, b, k * P:(k + 1) * P], identh[:, :])
                ins.then_inc(S("PmT_ps"), 1)

            def expert_up(gr):
                pe.wait_ge(S("cwA_lo"), gr + 1)
                pe.wait_ge(S("cwB_lo"), gr + 1)
                if gr >= 2:
                    pe.wait_ge(S("eh"), gr - 1)
                for q in range(GE):
                    e = GE * gr + q
                    W = EW16[2 * (gr % 3) + q // 2][:, q % 2]
                    for w in range(2):
                        for dc in range(DC):
                            for pw, px in PRODUCTS:
                                ins = mm(PS[:, gr % 2, 256 * w + q * CAP:256 * w + (q + 1) * CAP],
                                         W[:, pw, w * D + dc * P:w * D + (dc + 1) * P],
                                         Xp[:, px, dc, e * CAP:(e + 1) * CAP], dc == 0 and pw + px == 0, dc == 1 and pw == 1)
                ins.then_inc(S("eup_ps"), 1)

            def expert_down(gr):
                pe.wait_ge(S("eh"), gr + 1)
                if gr >= 2:
                    pe.wait_ge(S("yT"), gr - 1)
                for q in range(GE):
                    W = EW16[2 * (gr % 3) + q // 2][:, q % 2]
                    for dc in range(DC):
                        for pw, ph in PRODUCTS:
                            ins = mm(PS[:, 2 + gr % 2, dc * GS + q * CAP:dc * GS + (q + 1) * CAP],
                                     W[:, pw, 2 * D + dc * P:2 * D + (dc + 1) * P],
                                     eh[:, gr % 2, ph, q * CAP:(q + 1) * CAP], pw + ph == 0, pw == 1)
                ins.then_inc(S("y_ps"), 1)

            pe.wait_ge(S("Xp_hi"), 2 * len(ESPAN))
            pe.wait_ge(S("Xp_lo"), 2 * len(ESPAN))
            expert_up(0)
            for gr in range(NGR):
                if gr + 1 < NGR:
                    expert_up(gr + 1)
                for k in ([gr] if gr < NGR - 1 else range(gr, SC)):
                    turn_onehots(k)
                expert_down(gr)
            pe.wait_ge(S("yT"), NGR)
            pe.wait_ge(S("PmT"), SC)
            for k in range(SC):
                if k >= 4:
                    pe.wait_ge(S("y_lo"), k - 3)
                for dc in range(DC):
                    ins = tr(PS[:, 4 + k % 4, dc * P:(dc + 1) * P], yT[:, dc, k * P:(k + 1) * P])
                ins.then_inc(S("Y_ps"), 1)
            pe.wait_ge(S("hs"), NH * DC)
            for b in range(B):
                if b >= 4:
                    pe.wait_ge(S("x_updated"), 5 * B + b - 3)
                o_ = bank(b % 4, D)
                for ic in range(DC):
                    mm(o_, hs[:, ic, b * P:(b + 1) * P], WT[:, 2, ic, :], ic == 0, False)
                for k in range(SC):
                    for part in range(2):
                        if b == 0:
                            pe.wait_ge(S(("y_hi", "y_lo")[part]), k + 1)
                        ins = mm(o_, PmT[:, k, b * P:(b + 1) * P], Y2[:, part, k, :], False, k == SC - 1 and part == 1)
                ins.then_inc(S("e1_out"), 1)


_INS = ['x', 'fside_S2_0', 'ctx_2048', 'mask_SxS2_bc0', 'mask_BxS2_bk0', 'L0_attn_Wq', 'L0_attn_Wk', 'L0_attn_Wv',
        'L0_attn_Wo', 'L0_attn_bo', 'L0_xattn_k', 'L0_ffn_shared_w1', 'L0_ffn_shared_b1', 'L0_ffn_shared_w2',
        'L0_ffn_shared_b2', 'L0_ffn_routed_w1', 'L0_ffn_routed_b1', 'L0_ffn_routed_w2', 'L0_ffn_routed_b2',
        'L0_ffn_centroids', 'L0_ffn_bias', 'L1_attn_Wq', 'L1_attn_bq', 'L1_attn_Wk', 'L1_attn_bk', 'L1_attn_Wv',
        'L1_attn_bv', 'L1_attn_Wo', 'L1_attn_bo', 'L1_xattn_Wq', 'L1_xattn_bq', 'L1_xattn_Wk', 'L1_xattn_bk',
        'L1_xattn_Wv', 'L1_xattn_bv', 'L1_xattn_Wo', 'L1_xattn_bo', 'L1_ffn_router_w', 'L1_ffn_e_bias',
        'L1_ffn_W_gate', 'L1_ffn_W_up', 'L1_ffn_W_down', 'L1_ffn_shared_gate', 'L1_ffn_shared_up',
        'L1_ffn_shared_down']


def kernel(**inputs):
    import numpy as _np
    import concourse.bacc as _bacc
    from concourse import mybir as _mybir
    from concourse.bass_utils import run_bass_kernel_spmd as _run

    nc = _bacc.Bacc("TRN2", target_bir_lowering=False, num_devices=1)
    arrays, args = {}, {}
    for name in _INS:
        a = _np.ascontiguousarray(inputs[name])
        arrays[f"in_{name}_dram"] = a
        args[name] = nc.dram_tensor(f"in_{name}_dram", a.shape, _mybir.dt.from_np(a.dtype), kind="ExternalInput").ap()
    out = nc.dram_tensor("out_0_dram", (B, P, D), _mybir.dt.float32, kind="ExternalOutput").ap()
    decoder_kernel(nc, args, out)
    r = _run(nc, [arrays], core_ids=[0])
    return r.results[0]["out_0_dram"]
```
